# Optimizing a Trainium2 kernel written in Bass

```python
import numpy as np
import jax
import jax.numpy as jnp

def _softmax(x, axis=-1):
    return jax.nn.softmax(x, axis=axis)

def _gelu(x):
    return jax.nn.gelu(x, approximate=True)

def _silu(x):
    return jax.nn.silu(x)

def _sigmoid(x):
    return jax.nn.sigmoid(x)

def _layernorm(x, axis=-1, eps=1e-05):
    m = jnp.mean(x, axis=axis, keepdims=True)
    v = jnp.var(x, axis=axis, keepdims=True)
    return (x - m) / jnp.sqrt(v + eps)

def _scatter_add(tgt, idx, src, axis=0):
    return tgt.at[idx].add(src)

def _segment_sum(src, seg, n):
    return jax.ops.segment_sum(src, seg, n)
kernel_name = 'mk_gnn_ffn_d2_gnn_r32_bdd3d2'

def setup_inputs(seed: int=0):
    np.random.seed(seed)
    _w = jnp.asarray

    def _rec_inputs():
        import jax
        import jax.numpy as jnp
        _gk = jax.random.key(seed)
        x = -0.0002928 + 1 * jax.random.normal(jax.random.fold_in(_gk, 1), (256, 512), jnp.float32)
        src = jax.random.randint(jax.random.fold_in(_gk, 2), (8192,), 0, 256, jnp.int32)
        dst = jnp.minimum((256 * jax.random.uniform(jax.random.fold_in(_gk, 3), (8192,)) ** 2.0).astype(jnp.int32), 8191)
        _o = jnp.argsort(dst, stable=True)
        src = src[_o]
        dst = dst[_o]
        return (x, src, dst)
    x, src, dst = _rec_inputs()

    def _L0_gnn_setup():
        import jax, jax.numpy as jnp
        import numpy as np
        N_NODES = 256
        N_EDGES = 8192
        D_IN = 512
        D_OUT = 512
        key = jax.random.key(seed)
        k1, k2, k3 = jax.random.split(key, 3)
        x = jax.random.normal(k1, (N_NODES, D_IN), dtype=jnp.float32)
        edge_index = jax.random.randint(k2, (2, N_EDGES), 0, N_NODES, dtype=jnp.int64)
        weight = jax.random.normal(k3, (D_IN, D_OUT), dtype=jnp.float32)
        bias = jnp.zeros((D_OUT,), dtype=jnp.float32)
        return {'x': x, 'edge_index': edge_index, 'weight': weight, 'bias': bias}
    _L0_gnn_all = _L0_gnn_setup()
    _L0_gnn_in = {k: v for k, v in _L0_gnn_all.items() if k in ('weight', 'bias')}
    del _L0_gnn_all

    def _L0_ffn_setup():
        import jax, jax.numpy as jnp
        import numpy as np
        DIM = 512
        INTER = 64
        N_SHARED = 2
        N_ROUTED = 64
        TOPK = 6
        ROUTE_SCALE = 1.0
        B, T = (2, 512)
        key = jax.random.key(seed)
        ks = jax.random.split(key, 5)
        E = N_SHARED + N_ROUTED
        x = jax.random.normal(ks[0], (B, T, DIM), jnp.float32)
        g_w = jax.random.normal(ks[1], (N_ROUTED, DIM), jnp.float32) * 0.02
        gate_bias = jnp.ones((N_ROUTED,), jnp.float32)
        w1 = jax.random.normal(ks[2], (E, DIM, INTER), jnp.float32) * 0.02
        w2 = jax.random.normal(ks[3], (E, INTER, DIM), jnp.float32) * 0.02
        w3 = jax.random.normal(ks[4], (E, DIM, INTER), jnp.float32) * 0.02
        return {'x': x, 'g_w': g_w, 'gate_bias': gate_bias, 'w1': w1, 'w2': w2, 'w3': w3}
    _L0_ffn_all = _L0_ffn_setup()
    _L0_ffn_in = {k: v for k, v in _L0_ffn_all.items() if k in ('g_w', 'gate_bias', 'w1', 'w2', 'w3')}
    del _L0_ffn_all

    def _L1_gnn_setup():
        import jax, jax.numpy as jnp
        import numpy as np
        N = 50000
        E = 12500
        D = 512

        def sage_conv(x, edge_index, W_l, W_r, b):
            src, dst = (edge_index[0], edge_index[1])
            n = x.shape[0]
            msg = x[src]
            agg = jax.ops.segment_sum(msg, dst, num_segments=n)
            deg = jax.ops.segment_sum(jnp.ones((msg.shape[0],), x.dtype), dst, num_segments=n)
            mean = agg / jnp.maximum(deg, 1.0)[:, None]
            return mean @ W_l + x @ W_r + b
        key = jax.random.key(seed)
        k_x, k_e, k_wl, k_wr = jax.random.split(key, 4)
        x = jax.random.normal(k_x, (N, D), dtype=jnp.float32)
        edge_index = jax.random.randint(k_e, (2, E), 0, N, dtype=jnp.int32)
        scale = 1.0 / np.sqrt(D).astype(np.float32)
        W_l = jax.random.normal(k_wl, (D, D), dtype=jnp.float32) * scale
        W_r = jax.random.normal(k_wr, (D, D), dtype=jnp.float32) * scale
        b = jnp.zeros((D,), dtype=jnp.float32)
        return {'x': x, 'edge_index': edge_index, 'W_l': W_l, 'W_r': W_r, 'b': b}
    _L1_gnn_all = _L1_gnn_setup()
    _L1_gnn_in = {k: v for k, v in _L1_gnn_all.items() if k in ('W_l', 'W_r', 'b')}
    del _L1_gnn_all

    def _L1_ffn_setup():
        import jax, jax.numpy as jnp
        import numpy as np
        B, T, C = (8, 1024, 512)
        H = 1024
        G, EG = (2, 4)
        E = G * EG
        K = 2
        LN_EPS = 1e-05

        def _swiglu(x):
            a, b = jnp.split(x, 2, axis=-1)
            return jax.nn.silu(a) * b
        key = jax.random.key(seed)
        ks = jax.random.split(key, 8)
        n = lambda k, shape, s: jax.random.normal(k, shape, dtype=jnp.float32) * s
        return {'x': n(ks[0], (B, T, C), 1.0), 'ln_scale': jnp.ones((C,), jnp.float32), 'ln_bias': jnp.zeros((C,), jnp.float32), 'shared_in_w': n(ks[1], (2 * H, C), 0.02), 'shared_out_w': n(ks[2], (C, H), 0.02), 'shared_out_b': jnp.zeros((C,), jnp.float32), 'expert_in_w': n(ks[3], (2 * H, C), 0.02), 'expert_out_weight': n(ks[4], (E, C, H), 0.02), 'expert_out_bias': jnp.zeros((E, C), jnp.float32), 'group_gate_w': n(ks[5], (G, C), 0.02), 'expert_gate_w': n(ks[6], (E, C), 0.02), 'group_bias': jnp.zeros((G,), jnp.float32), 'expert_bias': jnp.zeros((E,), jnp.float32)}
    _L1_ffn_all = _L1_ffn_setup()
    _L1_ffn_in = {k: v for k, v in _L1_ffn_all.items() if k in ('ln_scale', 'ln_bias', 'shared_in_w', 'shared_out_w', 'shared_out_b', 'expert_in_w', 'expert_out_weight', 'expert_out_bias', 'group_gate_w', 'expert_gate_w', 'group_bias', 'expert_bias')}
    del _L1_ffn_all
    return {'x': x, 'src': src, 'dst': dst, 'L0_gnn_weight': _L0_gnn_in['weight'], 'L0_gnn_bias': _L0_gnn_in['bias'], 'L0_ffn_g_w': _L0_ffn_in['g_w'], 'L0_ffn_gate_bias': _L0_ffn_in['gate_bias'], 'L0_ffn_w1': _L0_ffn_in['w1'], 'L0_ffn_w2': _L0_ffn_in['w2'], 'L0_ffn_w3': _L0_ffn_in['w3'], 'L1_gnn_W_l': _L1_gnn_in['W_l'], 'L1_gnn_W_r': _L1_gnn_in['W_r'], 'L1_gnn_b': _L1_gnn_in['b'], 'L1_ffn_ln_scale': _L1_ffn_in['ln_scale'], 'L1_ffn_ln_bias': _L1_ffn_in['ln_bias'], 'L1_ffn_shared_in_w': _L1_ffn_in['shared_in_w'], 'L1_ffn_shared_out_w': _L1_ffn_in['shared_out_w'], 'L1_ffn_shared_out_b': _L1_ffn_in['shared_out_b'], 'L1_ffn_expert_in_w': _L1_ffn_in['expert_in_w'], 'L1_ffn_expert_out_weight': _L1_ffn_in['expert_out_weight'], 'L1_ffn_expert_out_bias': _L1_ffn_in['expert_out_bias'], 'L1_ffn_group_gate_w': _L1_ffn_in['group_gate_w'], 'L1_ffn_expert_gate_w': _L1_ffn_in['expert_gate_w'], 'L1_ffn_group_bias': _L1_ffn_in['group_bias'], 'L1_ffn_expert_bias': _L1_ffn_in['expert_bias']}

def reference(x, src, dst, L0_gnn_weight, L0_gnn_bias, L0_ffn_g_w, L0_ffn_gate_bias, L0_ffn_w1, L0_ffn_w2, L0_ffn_w3, L1_gnn_W_l, L1_gnn_W_r, L1_gnn_b, L1_ffn_ln_scale, L1_ffn_ln_bias, L1_ffn_shared_in_w, L1_ffn_shared_out_w, L1_ffn_shared_out_b, L1_ffn_expert_in_w, L1_ffn_expert_out_weight, L1_ffn_expert_out_bias, L1_ffn_group_gate_w, L1_ffn_expert_gate_w, L1_ffn_group_bias, L1_ffn_expert_bias):
    import jax
    import jax.numpy as jnp

    def _L0_gnn_ref(x, edge_index, weight, bias):
        import jax, jax.numpy as jnp
        import numpy as np
        N_NODES = 256
        N_EDGES = 8192
        D_IN = 512
        D_OUT = 512
        n = x.shape[0]
        adj = jnp.zeros((n, n), dtype=x.dtype)
        adj = adj.at[edge_index[0], edge_index[1]].set(1.0)
        adj = adj.at[edge_index[1], edge_index[0]].set(1.0)
        adj = adj + jnp.eye(n, dtype=x.dtype)
        deg = jnp.sum(adj, axis=1)
        dinv = 1.0 / jnp.sqrt(deg)
        adj = adj * dinv[:, None] * dinv[None, :]
        return adj @ (x @ weight) + bias

    def _L0_ffn_ref(x, g_w, gate_bias, w1, w2, w3):
        import jax, jax.numpy as jnp
        import numpy as np
        DIM = 512
        INTER = 64
        N_SHARED = 2
        N_ROUTED = 64
        TOPK = 6
        ROUTE_SCALE = 1.0
        B, T = (2, 512)
        Bx, Tx, C = x.shape
        K = TOPK + N_SHARED
        scores = jnp.einsum('btd,ed->bte', x, g_w)
        scores = jax.nn.softmax(scores.astype(jnp.float32), axis=-1)
        _, idx = jax.lax.top_k(scores + gate_bias, TOPK)
        rweights = jnp.take_along_axis(scores, idx, axis=-1) * ROUTE_SCALE
        rweights = rweights.astype(x.dtype)
        shared_idx = jnp.broadcast_to(jnp.arange(N_SHARED), (Bx, Tx, N_SHARED))
        expert_idx = jnp.concatenate([shared_idx, idx + N_SHARED], axis=-1)
        comb_w = jnp.concatenate([jnp.ones((Bx, Tx, N_SHARED), x.dtype), rweights], axis=-1)
        flat_idx = expert_idx.reshape(-1)
        x_rep = jnp.broadcast_to(x[:, :, None, :], (Bx, Tx, K, C)).reshape(-1, C)
        h1 = jnp.einsum('nd,nde->ne', x_rep, w1[flat_idx])
        h3 = jnp.einsum('nd,nde->ne', x_rep, w3[flat_idx])
        out = jnp.einsum('ne,ned->nd', jax.nn.silu(h1) * h3, w2[flat_idx])
        out = out * comb_w.reshape(-1, 1)
        return out.reshape(Bx, Tx, K, C).sum(axis=2)

    def _L1_gnn_ref(x, edge_index, W_l, W_r, b):
        import jax, jax.numpy as jnp
        import numpy as np
        N = 50000
        E = 12500
        D = 512

        def sage_conv(x, edge_index, W_l, W_r, b):
            src, dst = (edge_index[0], edge_index[1])
            n = x.shape[0]
            msg = x[src]
            agg = jax.ops.segment_sum(msg, dst, num_segments=n)
            deg = jax.ops.segment_sum(jnp.ones((msg.shape[0],), x.dtype), dst, num_segments=n)
            mean = agg / jnp.maximum(deg, 1.0)[:, None]
            return mean @ W_l + x @ W_r + b
        return sage_conv(x, edge_index, W_l, W_r, b)

    def _L1_ffn_ref(x, ln_scale, ln_bias, shared_in_w, shared_out_w, shared_out_b, expert_in_w, expert_out_weight, expert_out_bias, group_gate_w, expert_gate_w, group_bias, expert_bias):
        import jax, jax.numpy as jnp
        import numpy as np
        B, T, C = (8, 1024, 512)
        H = 1024
        G, EG = (2, 4)
        E = G * EG
        K = 2
        LN_EPS = 1e-05

        def _swiglu(x):
            a, b = jnp.split(x, 2, axis=-1)
            return jax.nn.silu(a) * b
        Bx, Tx, Cx = x.shape
        S = Bx * Tx
        flat = x.reshape(S, Cx)
        mu = flat.mean(-1, keepdims=True)
        var = ((flat - mu) ** 2).mean(-1, keepdims=True)
        flat = (flat - mu) * jax.lax.rsqrt(var + LN_EPS) * ln_scale + ln_bias
        h_shared = _swiglu(flat @ shared_in_w.T)
        out_shared = h_shared @ shared_out_w.T + shared_out_b
        g_logits = flat @ group_gate_w.T + group_bias
        g_idx = jnp.argmax(g_logits, axis=-1)
        e_logits = (flat @ expert_gate_w.T).reshape(S, G, EG)
        e_sel = jnp.take_along_axis(e_logits, g_idx[:, None, None], axis=1)[:, 0, :]
        e_sel = e_sel + expert_bias.reshape(G, EG)[g_idx]
        e_probs = jax.nn.softmax(e_sel, axis=-1)
        topv, topi = jax.lax.top_k(e_probs, K)
        topv = topv / (topv.sum(-1, keepdims=True) + 1e-08)
        disp = g_idx[:, None] * EG + topi
        h_expert = _swiglu(flat @ expert_in_w.T)
        rows = jnp.arange(S)[:, None]
        comb = jnp.zeros((S, E), flat.dtype).at[rows, disp].add(topv)
        cnt = jnp.zeros((S, E), flat.dtype).at[rows, disp].add(1.0)
        routed = cnt @ expert_out_bias
        for e in range(E):
            routed = routed + comb[:, e:e + 1] * (h_expert @ expert_out_weight[e].T)
        return (out_shared + routed).reshape(Bx, Tx, Cx)
    edge_index = jnp.stack([src, dst])
    x = x + _L0_gnn_ref(_layernorm(x, axis=-1), edge_index, L0_gnn_weight, L0_gnn_bias)
    x = x + _L0_ffn_ref(_layernorm(x, axis=-1)[None], L0_ffn_g_w, L0_ffn_gate_bias, L0_ffn_w1, L0_ffn_w2, L0_ffn_w3)[0]
    x = x + _L1_gnn_ref(_layernorm(x, axis=-1), edge_index, L1_gnn_W_l, L1_gnn_W_r, L1_gnn_b)
    x = x + _L1_ffn_ref(_layernorm(x, axis=-1)[None], L1_ffn_ln_scale, L1_ffn_ln_bias, L1_ffn_shared_in_w, L1_ffn_shared_out_w, L1_ffn_shared_out_b, L1_ffn_expert_in_w, L1_ffn_expert_out_weight, L1_ffn_expert_out_bias, L1_ffn_group_gate_w, L1_ffn_expert_gate_w, L1_ffn_group_bias, L1_ffn_expert_bias)[0]
    return x

_drawn_inputs = setup_inputs


def setup_inputs(seed=0):
    import zlib

    import numpy as np

    out = dict(_drawn_inputs(seed))
    spreads = {'L0_gnn_bias': (0.0, 0.1),
     'L0_ffn_gate_bias': (1.0, 0.6),
     'L1_gnn_b': (0.0, 0.624),
     'L1_ffn_ln_scale': (1.0, 0.6),
     'L1_ffn_ln_bias': (0.0, 0.603),
     'L1_ffn_shared_out_b': (0.0, 0.921),
     'L1_ffn_expert_out_bias': (0.0, 0.678),
     'L1_ffn_group_bias': (0.0, 0.8),
     'L1_ffn_expert_bias': (0.0, 0.4)}
    factors = {'L0_ffn_g_w': 8.0,
     'L0_ffn_w1': 6.281,
     'L0_ffn_w2': 6.323,
     'L0_ffn_w3': 6.173,
     'L1_ffn_expert_in_w': 3.47,
     'L1_ffn_expert_out_weight': 3.417,
     'L1_ffn_shared_in_w': 3.852,
     'L1_ffn_shared_out_w': 3.811}
    for name, (base, spread) in spreads.items():
        noise = np.random.default_rng([zlib.crc32(name.encode()), seed]).standard_normal(out[name].shape)
        drawn = base * np.exp(spread * noise) if base else spread * noise
        out[name] = jnp.asarray(drawn.astype(out[name].dtype))
    for name, factor in factors.items():
        out[name] = (out[name] * factor).astype(out[name].dtype)
    return out
```

```python
from contextlib import ExitStack

import concourse.bass as bass
from concourse import mybir

F32 = mybir.dt.float32
F32R = mybir.dt.float32r
BF16 = mybir.dt.bfloat16
I32 = mybir.dt.int32
U32 = mybir.dt.uint32
ALU = mybir.AluOpType
ACT = mybir.ActivationFunctionType
AX = mybir.AxisListType

P = 128
TOKENS, FEATURES, EDGES = 256, 512, 8192
TILES = TOKENS // P
CHUNKS = FEATURES // P
EDGE_COLS = EDGES // P
LN_EPS = 1e-5

EXPERTS, TOP_K, PAIRS, ROUTED_PAIRS = 64, 6, 33, 32
UNITS, HIDDEN_CHUNKS, EXPERTS1, GROUPS = 16, 8, 8, 2
GATES1 = EXPERTS1 + GROUPS

SLOTS = 4
SLAB_W = 2048
PAIR_W = 1536
UNIT_W = 1024
GCN_SLAB = 0
PAIR_SLAB = 1
SAGE_R_SLAB = PAIR_SLAB + PAIRS
SAGE_L_SLAB = SAGE_R_SLAB + 1
IN_SLAB = SAGE_L_SLAB + 1
IN_SLABS = UNITS // 2
OUT_SLAB = IN_SLAB + IN_SLABS
OUT_SLABS = 2 + 2 * EXPERTS1
SLABS = OUT_SLAB + OUT_SLABS

BLOCK = 8
BLOCKS = EDGE_COLS // BLOCK
LOOP_FIRST, LOOP_ROUNDS = 2, 7
LOOP_END = LOOP_FIRST + LOOP_ROUNDS * SLOTS

BIG = 1e30


def pool_makes_low(s):
    return s < SLOTS or IN_SLAB < s < IN_SLAB + SLOTS


def slab_width(s):
    return PAIR_W if PAIR_SLAB <= s < SAGE_R_SLAB else SLAB_W


def used_value(s):
    return s + 1 if s < IN_SLAB else s + 1 - IN_SLABS


def build(nc, x_in, src_in, dst_in, gcn_w_in, gcn_b_in, pairs_in, gates_in, gate_bias_in,
          sage_r_in, sage_l_in, sage_b_in, ln_affine_in, units_in, outs_in, out_bias_in,
          gate1_bias_in, out):
    with ExitStack() as ctx:
        def sb(name, shape, dt=F32):
            return ctx.enter_context(nc.sbuf_tensor(name, shape, dt))

        def sem(name):
            return ctx.enter_context(nc.semaphore(name))

        raw = [sb(f"raw{i}", [P, SLAB_W]) for i in range(SLOTS)]
        w_hi = [sb(f"w_hi{i}", [P, SLAB_W], F32R) for i in range(SLOTS)]
        w_lo = [sb(f"w_lo{i}", [P, SLAB_W], F32R) for i in range(SLOTS)]
        GATE_W = CHUNKS * (EXPERTS + GATES1)
        gates = sb("gates", [P, GATE_W])
        gates_hi = sb("gates_hi", [P, GATE_W], F32R)
        gates_lo = sb("gates_lo", [P, GATE_W], F32R)
        gcn_b = sb("gcn_b", [P, FEATURES])
        sage_b = sb("sage_b", [P, FEATURES])
        gate_bias = sb("gate_bias", [P, EXPERTS])
        gate1_bias = sb("gate1_bias", [P, GATES1])
        ln_affine = sb("ln_affine", [P, 2, CHUNKS])
        out_bias = sb("out_bias", [EXPERTS1 + 1, FEATURES])
        ident = sb("ident", [P, P])
        diag = sb("diag", [P, TILES, TOKENS])
        iota_i = sb("iota_i", [P, TOKENS], I32)
        iota_b = sb("iota_b", [P, TOKENS], BF16)
        iota_f = sb("iota_f", [P, EXPERTS])
        minus_half = sb("minus_half", [P, TILES])
        pair_sel_f = sb("pair_sel_f", [4, P])
        pair_sel = sb("pair_sel", [4, P], F32R)
        edges_i = sb("edges_i", [P, 2, EDGE_COLS], I32)
        edges_f = sb("edges_f", [P, 2, EDGE_COLS])
        hot_src = sb("hot_src", [P, BLOCK, TOKENS], BF16)
        hot_dst = sb("hot_dst", [P, BLOCK, TOKENS], BF16)
        count_t = sb("count_t", [P, TILES, TOKENS])
        adj = sb("adj", [P, TILES, TOKENS])
        deg = sb("deg", [P, TILES])
        dinv = sb("dinv", [P, TILES])
        in_deg = sb("in_deg", [P, TILES])
        rdeg = sb("rdeg", [P, TILES])
        x = sb("x", [P, TILES, FEATURES])
        resid = sb("resid", [P, TILES, FEATURES])
        z = sb("z", [P, TILES, FEATURES])
        zT = z[:].rearrange("p t f -> p (t f)").rearrange("p (c n) -> p c n", c=CHUNKS)
        zT_hi = sb("zT_hi", [P, CHUNKS, TOKENS], F32R)
        zT_lo = sb("zT_lo", [P, CHUNKS, TOKENS], F32R)
        aggT_hi = sb("aggT_hi", [P, CHUNKS, TOKENS], F32R)
        aggT_lo = sb("aggT_lo", [P, CHUNKS, TOKENS], F32R)
        u = sb("u", [P, TILES, FEATURES])
        z1 = u
        stats = sb("stats", [P, TILES, 6])
        mean_var = sb("mean_var", [P, TILES, 2])
        var_eps = sb("var_eps", [P, TILES])
        rstd = sb("rstd", [P, TILES])
        top = sb("top", [P, TILES, 8])
        top_i = sb("top_i", [P, TILES, 8], U32)
        top_f = sb("top_f", [P, TILES, 8])
        neg_max = sb("neg_max", [P, TILES])
        exp_sum = sb("exp_sum", [P, TILES])
        exp_rec = sb("exp_rec", [P, TILES])
        probs = sb("probs", [P, TILES, EXPERTS])
        picked = sb("picked", [P, TILES, EXPERTS])
        hits = sb("hits", [P, TILES, TOP_K, EXPERTS])
        comb = sb("comb", [P, TILES, EXPERTS])
        comb_parts = sb("comb_parts", [P, TILES, 2, EXPERTS], F32R)
        combT = sb("combT", [P, TOKENS], F32R)
        logits1 = sb("logits1", [P, TILES, GATES1])
        group_on = sb("group_on", [P, TILES, GROUPS])
        group_pen = sb("group_pen", [P, TILES, GROUPS])
        e1 = sb("e1", [P, TILES, EXPERTS1])
        p1 = sb("p1", [P, TILES, EXPERTS1])
        hits1 = sb("hits1", [P, TILES, 2, EXPERTS1])
        count1 = sb("count1", [P, TILES, P])
        count1T = sb("count1T", [EXPERTS1 + 1, TOKENS])
        comb1 = sb("comb1", [P, TILES, EXPERTS1])
        silu = [sb(f"silu{i}", [P, TOKENS]) for i in range(2)]
        glu = [sb(f"glu{i}", [P, TOKENS]) for i in range(2)]
        g = [sb(f"g{i}", [P, TOKENS]) for i in range(2)]
        g_hi = [sb(f"g_hi{i}", [P, TOKENS], F32R) for i in range(2)]
        g_lo = [sb(f"g_lo{i}", [P, TOKENS], F32R) for i in range(2)]
        hid = sb("hid", [P, 2 * UNITS * TOKENS], F32R)
        hid_hi, hid_lo = hid[:, 0:UNITS * TOKENS], hid[:, UNITS * TOKENS:]
        comb_rows = hid[0:4, 0:ROUTED_PAIRS * TOKENS]

        bank = [ctx.enter_context(nc.psum_tensor(f"bank{i}", [P, 512], F32)) for i in range(8)]
        y = bank[0:2]
        gate_ps = bank[2:4]
        up_ps = bank[4:6]
        misc = bank[6:8]

        edges_in, x_in_s, consts_in = sem("edges_in"), sem("x_in"), sem("consts_in")
        raw_in = [sem(f"raw_in{i}") for i in range(SLOTS)]
        hi_done, dve_lo_done, pool_lo_done = sem("hi_done"), sem("dve_lo_done"), sem("pool_lo_done")
        slab_used = sem("slab_used")
        gates_hi_done, gates_lo_done = sem("gates_hi_done"), sem("gates_lo_done")
        pool_const, pool_chain = sem("pool_const"), sem("pool_chain")
        pair_sel_done = sem("pair_sel_done")
        bias_added = sem("bias_added")
        var_ready, rstd_ready, z_ready = sem("var_ready"), sem("rstd_ready"), sem("z_ready")
        transposed, zT_hi_done, zT_lo_done = sem("transposed"), sem("zT_hi_done"), sem("zT_lo_done")
        affine_done = sem("affine_done")
        hot_ready, hot_used = sem("hot_ready"), sem("hot_used")
        count_copied, count_flipped = sem("count_copied"), sem("count_flipped")
        deg_ready, dinv_ready, adj_ready = sem("deg_ready"), sem("dinv_ready"), sem("adj_ready")
        u_ps_ready, u_ready, gcn_ready = sem("u_ps_ready"), sem("u_ready"), sem("gcn_ready")
        logits_ready, max_ready, exp_ready = sem("logits_ready"), sem("max_ready"), sem("exp_ready")
        comb_ready, comb_hi_done, comb_lo_done = sem("comb_ready"), sem("comb_hi_done"), sem("comb_lo_done")
        combT_ps, combT_ready, rows_in = sem("combT_ps"), sem("combT_ready"), sem("rows_in")
        up_ready, silu_done, glu_done = sem("up_ready"), sem("silu_done"), sem("glu_done")
        spread, g_done, g_hi_done, g_lo_done = sem("spread"), sem("g_done"), sem("g_hi_done"), sem("g_lo_done")
        agg_ready = sem("agg_ready")
        sage_ready = sem("sage_ready")
        exp1_in, exp1_done = sem("exp1_in"), sem("exp1_done")
        count1_ready, count1T_ps, count1T_ready = sem("count1_ready"), sem("count1T_ps"), sem("count1T_ready")
        shared_ready, expert_ready, added = sem("shared_ready"), sem("expert_ready"), sem("added")
        dve_chain = sem("dve_chain")
        result_ready, stored = sem("result_ready"), sem("stored")

        block = ctx.enter_context(nc.Block())

        def low_wait(eng, s, first=None):
            at = s if first is None else first
            if pool_makes_low(at):
                eng.wait_ge(pool_lo_done, s + 1 if at < SLOTS else s - IN_SLAB + SLOTS)
            elif at <= IN_SLAB:
                eng.wait_ge(dve_lo_done, s - SLOTS + 1)
            else:
                eng.wait_ge(dve_lo_done, s - 2 * SLOTS + 2)

        @block.sync
        def _(sp):
            def load(slot, source, width):
                sp.dma_start(raw[slot][:, 0:width], source).then_inc(raw_in[slot], 16)

            sp.dma_start(edges_i[:, 0, :], src_in.rearrange("(p j) -> p j", p=P)).then_inc(edges_in, 16)
            sp.dma_start(edges_i[:, 1, :], dst_in.rearrange("(p j) -> p j", p=P)).then_inc(edges_in, 16)
            sp.dma_start(x[:], x_in.rearrange("(t p) f -> p t f", p=P)).then_inc(x_in_s, 16)
            load(0, gcn_w_in, SLAB_W)
            for s in range(PAIR_SLAB, 2 * SLOTS):
                if s >= SLOTS:
                    low_wait(sp, s - SLOTS)
                load(s % SLOTS, pairs_in[s - PAIR_SLAB], PAIR_W)
            with sp.Fori(0, 6) as i:
                for j in range(SLOTS):
                    s = 2 * SLOTS + SLOTS * i + j
                    low_wait(sp, s - SLOTS, first=SLOTS + j)
                    load(j, pairs_in[bass.ds(s - PAIR_SLAB, 1), :, :].rearrange("a p w -> p (a w)"), PAIR_W)
            for s in range(8 * SLOTS, 12 * SLOTS):
                low_wait(sp, s - SLOTS)
                if s < SAGE_R_SLAB:
                    load(s % SLOTS, pairs_in[s - PAIR_SLAB], PAIR_W)
                elif s == SAGE_R_SLAB:
                    load(s % SLOTS, sage_r_in, SLAB_W)
                elif s == SAGE_L_SLAB:
                    load(s % SLOTS, sage_l_in, SLAB_W)
                elif s < OUT_SLAB:
                    load(s % SLOTS, units_in[s - IN_SLAB], SLAB_W)
                else:
                    load(s % SLOTS, outs_in[s - OUT_SLAB], SLAB_W)
            with sp.Fori(0, 3) as i:
                for j in range(SLOTS):
                    s = 12 * SLOTS + SLOTS * i + j
                    low_wait(sp, s - SLOTS, first=11 * SLOTS + j)
                    load(j, outs_in[bass.ds(s - OUT_SLAB, 1), :, :].rearrange("a p w -> p (a w)"), SLAB_W)
            for s in range(15 * SLOTS, SLABS):
                low_wait(sp, s - SLOTS)
                load(s % SLOTS, outs_in[s - OUT_SLAB], SLAB_W)
            for t in range(TILES):
                sp.wait_ge(result_ready, t + 1)
                sp.dma_start(out[t * P:(t + 1) * P, :], resid[:, t, :]).then_inc(stored, 16)
            sp.wait_ge(stored, 16 * TILES)

        @block.gpsimd
        def _(pool):
            chain = [0]

            def link(ins):
                chain[0] += 1
                ins.then_inc(pool_chain, 1)
                pool.wait_ge(pool_chain, chain[0])

            link(nc.gpsimd.iota(iota_i[:], [[1, TOKENS]], base=0, channel_multiplier=0))
            nc.gpsimd.tensor_copy(iota_b[:], iota_i[:]).then_inc(pool_const, 1)
            link(nc.gpsimd.memset(ident[:], 0.0))
            nc.gpsimd.affine_select(out=ident[:], in_=ident[:], compare_op=ALU.not_equal, fill=1.0, base=0,
                                    pattern=[[-1, P]], channel_multiplier=1).then_inc(pool_const, 1)
            link(nc.gpsimd.memset(minus_half[:], -0.5))
            pool.wait_ge(var_ready, 1)
            nc.gpsimd.tensor_tensor(rstd[:], var_eps[:], minus_half[:], ALU.pow).then_inc(rstd_ready, 1)
            nc.gpsimd.tensor_copy(iota_f[:], iota_i[:, 0:EXPERTS]).then_inc(pool_const, 1)
            link(nc.gpsimd.memset(diag[:], 0.0))
            nc.gpsimd.affine_select(out=diag[:], in_=diag[:], compare_op=ALU.not_equal, fill=1.0, base=0,
                                    pattern=[[P, TILES], [-1, TOKENS]], channel_multiplier=1).then_inc(pool_const, 1)
            link(nc.gpsimd.memset(pair_sel_f[:], 1.0))
            link(nc.gpsimd.affine_select(out=pair_sel_f[:, 0:64], in_=pair_sel_f[:, 0:64], compare_op=ALU.is_ge,
                                         fill=0.0, base=1, pattern=[[0, 64]], channel_multiplier=-1))
            link(nc.gpsimd.affine_select(out=pair_sel_f[:, 64:P], in_=pair_sel_f[:, 64:P], compare_op=ALU.is_ge,
                                         fill=0.0, base=-2, pattern=[[0, 64]], channel_multiplier=1))
            nc.gpsimd.tensor_copy(pair_sel[:], pair_sel_f[:]).then_inc(pair_sel_done, 1)
            nc.gpsimd.memset(count1[:], 1.0).then_inc(pool_const, 1)

            def low(s, width):
                pool.wait_ge(hi_done, s + 1)
                nc.gpsimd.tensor_tensor(w_lo[s % SLOTS][:, 0:width], raw[s % SLOTS][:, 0:width],
                                        w_hi[s % SLOTS][:, 0:width].bitcast(F32), ALU.subtract).then_inc(pool_lo_done, 1)

            low(0, SLAB_W)
            pool.wait_ge(x_in_s, 16)
            pool.wait_ge(consts_in, 16 * 8)
            for t in range(TILES):
                nc.gpsimd.tensor_tensor(resid[:, t, :], x[:, t, :], gcn_b[:], ALU.add).then_inc(bias_added, 1)
            pool.wait_ge(gates_hi_done, 1)
            nc.gpsimd.tensor_tensor(gates_lo[:], gates[:], gates_hi[:].bitcast(F32), ALU.subtract).then_inc(gates_lo_done, 1)
            for s in range(PAIR_SLAB, SLOTS):
                low(s, PAIR_W)
            pool.wait_ge(deg_ready, TILES)
            nc.gpsimd.tensor_tensor(dinv[:], deg[:], minus_half[:], ALU.pow).then_inc(dinv_ready, 1)

            def inverse_root(n):
                pool.wait_ge(var_ready, n)
                nc.gpsimd.tensor_tensor(rstd[:], var_eps[:], minus_half[:], ALU.pow).then_inc(rstd_ready, 1)

            inverse_root(2)
            inverse_root(3)
            for t in range(TILES):
                nc.gpsimd.tensor_tensor(x[:, t, :], resid[:, t, :], sage_b[:], ALU.add).then_inc(bias_added, 1)
            low(IN_SLAB + 1, SLAB_W)
            low(IN_SLAB + 2, SLAB_W)
            inverse_root(4)
            inverse_root(5)
            low(IN_SLAB + 3, SLAB_W)

        @block.scalar
        def _(act):
            act.dma_start(gcn_b[:], gcn_b_in.partition_broadcast(P)).then_inc(consts_in, 16)
            act.dma_start(gates[:], gates_in).then_inc(consts_in, 16)
            act.dma_start(gate_bias[:], gate_bias_in.partition_broadcast(P)).then_inc(consts_in, 16)
            act.dma_start(sage_b[:], sage_b_in.partition_broadcast(P)).then_inc(consts_in, 16)
            act.dma_start(gate1_bias[:], gate1_bias_in.partition_broadcast(P)).then_inc(consts_in, 16)
            act.dma_start(ln_affine[:, 0, :], ln_affine_in[0]).then_inc(consts_in, 16)
            act.dma_start(ln_affine[:, 1, :], ln_affine_in[1]).then_inc(consts_in, 16)
            act.dma_start(out_bias[:], out_bias_in).then_inc(consts_in, 16)

            def high(s, slot, width, used=None):
                act.wait_ge(raw_in[slot], (s - slot) * (16 // SLOTS) + 16)
                if used is not None:
                    act.wait_ge(slab_used, used)
                nc.scalar.activation(w_hi[slot][:, 0:width], raw[slot][:, 0:width], ACT.Copy).then_inc(hi_done, 1)

            def split_transposed(n):
                for b in range(2):
                    act.wait_ge(transposed, 2 * n + b + 1)
                    nc.scalar.activation(zT_hi[:, 2 * b:2 * b + 2, :],
                                         misc[b][:].rearrange("p (c n) -> p c n", c=2), ACT.Copy).then_inc(zT_hi_done, 1)

            high(0, 0, SLAB_W)
            split_transposed(0)
            act.wait_ge(consts_in, 16 * 8)
            nc.scalar.activation(gates_hi[:], gates[:], ACT.Copy).then_inc(gates_hi_done, 1)
            for s in range(PAIR_SLAB, SLOTS):
                high(s, s, PAIR_W)
            for t in range(TILES):
                act.wait_ge(hot_used, EDGE_COLS)
                nc.scalar.activation(count_t[:, t, :], gate_ps[t][:, 0:TOKENS], ACT.Copy).then_inc(count_copied, 1)
            for t, ready in enumerate((u_ps_ready, slab_used)):
                act.wait_ge(ready, 1)
                nc.scalar.activation(u[:, t, :], y[t][:], ACT.Copy).then_inc(u_ready, 1)
            split_transposed(1)

            def act_silu(k, q):
                act.wait_ge(up_ready, k + 1)
                nc.scalar.activation(silu[q][:], gate_ps[q][:, 0:TOKENS], ACT.Silu).then_inc(silu_done, 1)

            def act_g_high(k, q, dest=None):
                act.wait_ge(g_done, k + 1)
                nc.scalar.activation(g_hi[q][:] if dest is None else dest, g[q][:], ACT.Copy).then_inc(g_hi_done, 1)

            for t in range(TILES):
                act.wait_ge(max_ready, 1)
                nc.scalar.activation(probs[:, t, :], misc[1][:, t * EXPERTS:(t + 1) * EXPERTS], ACT.Exp,
                                     bias=neg_max[:, t:t + 1], accum_out=exp_sum[:, t:t + 1]).then_inc(exp_ready, 1)
            act.wait_ge(comb_ready, 1)
            nc.scalar.activation(comb_parts[:, :, 0, :], comb[:], ACT.Copy).then_inc(comb_hi_done, 1)
            act.wait_ge(combT_ps, 1)
            nc.scalar.activation(combT[:], misc[0][:, 0:TOKENS], ACT.Copy).then_inc(combT_ready, 1)
            act.wait_ge(combT_ready, 1)
            for k in range(2):
                for part in range(2):
                    first = part * EXPERTS + k
                    row = 2 * k + part
                    act.dma_start(comb_rows[row:row + 1, :].bitcast(F32).rearrange("r (a n) -> r a n", n=TOKENS),
                                  combT[first:part * EXPERTS + EXPERTS:2, :].bitcast(F32)).then_inc(rows_in, 16)
            for p in range(LOOP_FIRST):
                act_silu(p, p % 2)
                act_g_high(p, p % 2)
                high(p + 4, (p + 4) % SLOTS, PAIR_W, used=p + 1)
            with act.Fori(0, LOOP_ROUNDS) as i:
                for j in range(SLOTS):
                    p = SLOTS * i + (LOOP_FIRST + j)
                    act_silu(p, j % 2)
                    act_g_high(p, j % 2)
                    high(p + 4, (LOOP_FIRST + j) % SLOTS, PAIR_W, used=p + 1)
            for p in range(LOOP_END, PAIRS):
                act_silu(p, p % 2)
                act_g_high(p, p % 2)
                high(p + 4, (p + 4) % SLOTS, slab_width(p + 4), used=p + 1)
            high(IN_SLAB + 1, (IN_SLAB + 1) % SLOTS, SLAB_W, used=used_value(IN_SLAB - 3))
            split_transposed(2)
            for b in range(2):
                act.wait_ge(agg_ready, b + 1)
                nc.scalar.activation(aggT_hi[:, 2 * b:2 * b + 2, :],
                                     gate_ps[b][:].rearrange("p (c n) -> p c n", c=2), ACT.Copy).then_inc(zT_hi_done, 1)
            for s in (IN_SLAB + 2, IN_SLAB + 3):
                high(s, s % SLOTS, SLAB_W, used=used_value(s - SLOTS))
            for b in range(2):
                act.wait_ge(affine_done, b + 1)
                nc.scalar.activation(zT_hi[:, 2 * b:2 * b + 2, :], zT[:, 2 * b:2 * b + 2, :], ACT.Copy).then_inc(zT_hi_done, 1)
            act.wait_ge(exp1_in, 1)
            nc.scalar.activation(p1[:], e1[:], ACT.Exp).then_inc(exp1_done, 1)
            with act.Fori(0, IN_SLABS // SLOTS) as i:
                for j in range(SLOTS):
                    for v in range(2):
                        unit = (2 * SLOTS) * i + (2 * j + v)
                        act_silu(PAIRS + unit, (PAIRS + v) % 2)
                        act_g_high(PAIRS + unit, (PAIRS + v) % 2, hid_hi[:, bass.ds(unit * TOKENS, TOKENS)])
                    high(SLOTS * i + (IN_SLAB + SLOTS + j), (IN_SLAB + j) % SLOTS, SLAB_W)
            act.wait_ge(count1T_ps, 1)
            nc.scalar.activation(count1T[:], misc[1][0:EXPERTS1 + 1, 0:TOKENS], ACT.Copy).then_inc(count1T_ready, 1)
            with act.Fori(0, 3) as i:
                for j in range(SLOTS):
                    high(SLOTS * i + (12 * SLOTS + j), j, SLAB_W, used=SLOTS * i + used_value(11 * SLOTS + j))
            for s in range(15 * SLOTS, SLABS):
                high(s, s % SLOTS, SLAB_W, used=used_value(s - SLOTS))

        @block.vector
        def _(dve):
            chain = [0]

            def link(ins):
                chain[0] += 1
                ins.then_inc(dve_chain, 1)
                dve.wait_ge(dve_chain, chain[0])

            def layer_norm(source, dest, n):
                for t in range(TILES):
                    last = nc.vector.bn_stats(stats[:, t, :], source[:, t, :])
                    if t == 0:
                        last.then_inc(dve_chain, 1)
                        chain[0] += 1
                link(last)
                for t in range(TILES):
                    last = nc.vector.bn_aggr(mean_var[:, t, :], stats[:, t, :])
                    if t == 0:
                        last.then_inc(dve_chain, 1)
                        chain[0] += 1
                link(last)
                nc.vector.tensor_scalar(var_eps[:], mean_var[:, :, 1], LN_EPS, None, ALU.add).then_inc(var_ready, 1)
                dve.wait_ge(rstd_ready, n)
                for t in range(TILES):
                    nc.vector.tensor_scalar(dest[:, t, :], source[:, t, :], mean_var[:, t, 0:1], rstd[:, t:t + 1],
                                            ALU.subtract, ALU.mult).then_inc(z_ready, 1)

            def low(s, slot, width):
                dve.wait_ge(hi_done, s + 1)
                nc.vector.tensor_tensor(w_lo[slot][:, 0:width], raw[slot][:, 0:width],
                                        w_hi[slot][:, 0:width].bitcast(F32), ALU.subtract).then_inc(dve_lo_done, 1)

            def low_transposed(n):
                for b in range(2):
                    dve.wait_ge(zT_hi_done, 2 * n + b + 1)
                    nc.vector.tensor_tensor(zT_lo[:, 2 * b:2 * b + 2, :],
                                            misc[b][:].rearrange("p (c n) -> p c n", c=2),
                                            zT_hi[:, 2 * b:2 * b + 2, :].bitcast(F32), ALU.subtract).then_inc(zT_lo_done, 1)

            dve.wait_ge(edges_in, 32)
            link(nc.vector.tensor_copy(edges_f[:], edges_i[:]))

            def hot_column(col, j):
                nc.vector.tensor_scalar(hot_src[:, j, :], iota_b[:], edges_f[:, 0, bass.ds(col, 1)], None, ALU.is_equal)
                nc.vector.tensor_scalar(hot_dst[:, j, :], iota_b[:], edges_f[:, 1, bass.ds(col, 1)], None,
                                        ALU.is_equal).then_inc(hot_ready, 1)

            dve.wait_ge(pool_const, 1)
            for j in range(BLOCK):
                hot_column(j, j)
            dve.wait_ge(x_in_s, 16)
            layer_norm(x, z, 1)
            with dve.Fori(0, BLOCKS - 1) as i:
                for j in range(BLOCK):
                    dve.wait_ge(hot_used, BLOCK * i + (j + 1))
                    hot_column(BLOCK * i + (BLOCK + j), j)
            low_transposed(0)
            dve.wait_ge(pool_const, 4)
            for t in range(TILES):
                dve.wait_ge(count_copied, t + 1)
                dve.wait_ge(count_flipped, t + 1)
                link(nc.vector.tensor_tensor(adj[:, t, :], up_ps[t][:, 0:TOKENS], count_t[:, t, :], ALU.add))
                nc.vector.scalar_tensor_tensor(adj[:, t, :], adj[:, t, :], 1.0, diag[:, t, :], ALU.min, ALU.add,
                                               accum_out=deg[:, t:t + 1]).then_inc(deg_ready, 1)
            for t in range(TILES):
                link(nc.vector.tensor_reduce(in_deg[:, t:t + 1], up_ps[t][:, 0:TOKENS], axis=AX.X, op=ALU.add))
            link(nc.vector.tensor_scalar(in_deg[:], in_deg[:], 1.0, None, ALU.max))
            link(nc.vector.reciprocal(rdeg[:], in_deg[:]))
            dve.wait_ge(dinv_ready, 1)
            for t in range(TILES):
                nc.vector.tensor_scalar(adj[:, t, :], adj[:, t, :], dinv[:, t:t + 1], None, ALU.mult).then_inc(adj_ready, 1)
            dve.wait_ge(bias_added, TILES)
            for t in range(TILES):
                dve.wait_ge(gcn_ready, t + 1)
                link(nc.vector.scalar_tensor_tensor(resid[:, t, :], gate_ps[t][:], dinv[:, t:t + 1], resid[:, t, :],
                                                    ALU.mult, ALU.add))
            layer_norm(resid, z, 2)
            low_transposed(1)

            dve.wait_ge(logits_ready, 1)
            scores = misc[1][:, 0:TILES * EXPERTS].rearrange("p (t e) -> p t e", e=EXPERTS)
            link(nc.vector.tensor_reduce(neg_max[:], scores, axis=AX.X, op=ALU.max))
            nc.vector.tensor_scalar(neg_max[:], neg_max[:], -1.0, None, ALU.mult).then_inc(max_ready, 1)
            dve.wait_ge(exp_ready, TILES)
            link(nc.vector.reciprocal(exp_rec[:], exp_sum[:]))
            for t in range(TILES):
                link(nc.vector.tensor_scalar(probs[:, t, :], probs[:, t, :], exp_rec[:, t:t + 1], None, ALU.mult))
                link(nc.vector.tensor_tensor(picked[:, t, :], probs[:, t, :], gate_bias[:], ALU.add))
                link(nc.vector.max(top[:, t, :], picked[:, t, :]))
                link(nc.vector.max_index(top_i[:, t, :], top[:, t, :], picked[:, t, :]))
            link(nc.vector.tensor_copy(top_f[:], top_i[:]))
            for t in range(TILES):
                link(nc.vector.tensor_tensor(hits[:, t, :, :],
                                             iota_f[:].unsqueeze(1).to_broadcast([P, TOP_K, EXPERTS]),
                                             top_f[:, t, 0:TOP_K].unsqueeze(2).to_broadcast([P, TOP_K, EXPERTS]),
                                             ALU.is_equal))
                link(nc.vector.tensor_reduce(picked[:, t, :], hits[:, t, :, :].rearrange("p k e -> p e k"),
                                             axis=AX.X, op=ALU.add))
            nc.vector.tensor_tensor(comb[:], probs[:], picked[:], ALU.mult).then_inc(comb_ready, 1)
            dve.wait_ge(comb_hi_done, 1)
            nc.vector.tensor_tensor(comb_parts[:, :, 1, :], comb[:], comb_parts[:, :, 0, :].bitcast(F32),
                                    ALU.subtract).then_inc(comb_lo_done, 1)

            def gated(k, q, weighted, dest=None, spread_at=None, glu_at=None):
                dve.wait_ge(silu_done, k + 1)
                if weighted:
                    nc.vector.tensor_tensor(glu[q][:], silu[q][:], up_ps[q][:, 0:TOKENS], ALU.mult).then_inc(glu_done, 1)
                    dve.wait_ge(spread, k)
                    dve.wait_ge(glu_done, k)
                    nc.vector.tensor_tensor(g[q][:], glu[q][:], misc[q][:, 0:TOKENS], ALU.mult).then_inc(g_done, 1)
                else:
                    nc.vector.tensor_tensor(g[q][:], silu[q][:], up_ps[q][:, 0:TOKENS], ALU.mult).then_inc(g_done, 1)
                dve.wait_ge(g_hi_done, k + 1)
                hi, lo = (g_hi[q][:], g_lo[q][:]) if dest is None else dest
                nc.vector.tensor_tensor(lo, g[q][:], hi.bitcast(F32), ALU.subtract).then_inc(g_lo_done, 1)

            for p in range(LOOP_FIRST):
                gated(p, p % 2, p > 0)
                low(p + 4, (p + 4) % SLOTS, PAIR_W)
            with dve.Fori(0, LOOP_ROUNDS) as i:
                for j in range(SLOTS):
                    p = SLOTS * i + (LOOP_FIRST + j)
                    gated(p, j % 2, True)
                    low(p + 4, (LOOP_FIRST + j) % SLOTS, PAIR_W)
            for p in range(LOOP_END, PAIRS):
                gated(p, p % 2, True)
                low(p + 4, (p + 4) % SLOTS, slab_width(p + 4))
            dve.wait_ge(slab_used, SAGE_R_SLAB)
            for t in range(TILES):
                link(nc.vector.tensor_tensor(resid[:, t, :], resid[:, t, :], y[t][:], ALU.add))

            layer_norm(resid, z, 3)
            low_transposed(2)
            for b in range(2):
                dve.wait_ge(zT_hi_done, 6 + b + 1)
                nc.vector.tensor_tensor(aggT_lo[:, 2 * b:2 * b + 2, :],
                                        gate_ps[b][:].rearrange("p (c n) -> p c n", c=2),
                                        aggT_hi[:, 2 * b:2 * b + 2, :].bitcast(F32), ALU.subtract).then_inc(zT_lo_done, 1)
            dve.wait_ge(bias_added, 2 * TILES)
            for t, (ready, value) in enumerate(((sage_ready, 1), (slab_used, SAGE_R_SLAB + 1))):
                dve.wait_ge(ready, value)
                link(nc.vector.tensor_tensor(x[:, t, :], x[:, t, :], up_ps[t][:], ALU.add))
            for t, (ready, value) in enumerate(((sage_ready, 2), (slab_used, SAGE_L_SLAB + 1))):
                dve.wait_ge(ready, value)
                link(nc.vector.scalar_tensor_tensor(resid[:, t, :], y[t][:], rdeg[:, t:t + 1], x[:, t, :],
                                                    ALU.mult, ALU.add))
            layer_norm(resid, z, 4)
            dve.wait_ge(z_ready, 4 * TILES)
            layer_norm(z, z1, 5)
            for b in range(2):
                dve.wait_ge(transposed, 6 + b + 1)
                for c in (2 * b, 2 * b + 1):
                    last = nc.vector.tensor_scalar(zT[:, c, :], misc[b][:, (c % 2) * TOKENS:(c % 2 + 1) * TOKENS],
                                                   ln_affine[:, 0, c:c + 1], ln_affine[:, 1, c:c + 1], ALU.mult, ALU.add)
                    if c % 2 == 0:
                        last.then_inc(dve_chain, 1)
                        chain[0] += 1
                last.then_inc(affine_done, 1)
            for b in range(2):
                dve.wait_ge(zT_hi_done, 8 + b + 1)
                nc.vector.tensor_tensor(zT_lo[:, 2 * b:2 * b + 2, :], zT[:, 2 * b:2 * b + 2, :],
                                        zT_hi[:, 2 * b:2 * b + 2, :].bitcast(F32), ALU.subtract).then_inc(zT_lo_done, 1)

            dve.wait_ge(logits_ready, 2)
            link(nc.vector.tensor_tensor(logits1[:],
                                         misc[0][:, 0:TILES * GATES1].rearrange("p (t e) -> p t e", e=GATES1),
                                         gate1_bias[:].unsqueeze(1).to_broadcast([P, TILES, GATES1]), ALU.add))
            nc.vector.tensor_tensor(group_on[:, :, 0], logits1[:, :, EXPERTS1], logits1[:, :, EXPERTS1 + 1],
                                    ALU.is_ge).then_inc(dve_chain, 1)
            chain[0] += 1
            link(nc.vector.tensor_tensor(group_on[:, :, 1], logits1[:, :, EXPERTS1 + 1], logits1[:, :, EXPERTS1],
                                         ALU.is_gt))
            link(nc.vector.tensor_scalar(group_pen[:], group_on[:], BIG, -BIG, ALU.mult, ALU.add))

            def spread_group(a, t):
                return a[:, t, :].unsqueeze(2).to_broadcast([P, GROUPS, EXPERTS1 // GROUPS])

            def by_group(a, t):
                return a[:, t, 0:EXPERTS1].rearrange("p (g e) -> p g e", g=GROUPS)

            for t in range(TILES):
                link(nc.vector.tensor_tensor(by_group(e1, t), by_group(logits1, t), spread_group(group_on, t), ALU.mult))
                link(nc.vector.tensor_tensor(by_group(e1, t), by_group(e1, t), spread_group(group_pen, t), ALU.add))
            link(nc.vector.tensor_reduce(neg_max[:], e1[:], axis=AX.X, op=ALU.max))
            nc.vector.tensor_tensor(e1[:], e1[:], neg_max[:].unsqueeze(2).to_broadcast([P, TILES, EXPERTS1]),
                                    ALU.subtract).then_inc(exp1_in, 1)
            dve.wait_ge(exp1_done, 1)
            link(nc.vector.tensor_reduce(exp_sum[:], p1[:], axis=AX.X, op=ALU.add))
            link(nc.vector.reciprocal(exp_rec[:], exp_sum[:]))
            link(nc.vector.tensor_tensor(p1[:], p1[:], exp_rec[:].unsqueeze(2).to_broadcast([P, TILES, EXPERTS1]), ALU.mult))
            link(nc.vector.tensor_scalar(group_pen[:], group_on[:], -1.0, None, ALU.add))
            for t in range(TILES):
                link(nc.vector.tensor_tensor(by_group(e1, t), by_group(p1, t), spread_group(group_pen, t), ALU.add))
                link(nc.vector.max(top[:, t, :], e1[:, t, :]))
                link(nc.vector.max_index(top_i[:, t, :], top[:, t, :], e1[:, t, :]))
            link(nc.vector.tensor_copy(top_f[:], top_i[:]))
            for t in range(TILES):
                link(nc.vector.tensor_tensor(hits1[:, t, :, :],
                                             iota_f[:, 0:EXPERTS1].unsqueeze(1).to_broadcast([P, 2, EXPERTS1]),
                                             top_f[:, t, 0:2].unsqueeze(2).to_broadcast([P, 2, EXPERTS1]), ALU.is_equal))
            dve.wait_ge(pool_const, 5)
            nc.vector.tensor_tensor(count1[:, :, 0:EXPERTS1], hits1[:, :, 0, :], hits1[:, :, 1, :],
                                    ALU.add).then_inc(count1_ready, 1)
            dve.wait_ge(count1_ready, 1)
            link(nc.vector.scalar_tensor_tensor(exp_sum[:], top[:, :, 0], 1e-8, top[:, :, 1], ALU.add, ALU.add))
            link(nc.vector.reciprocal(exp_rec[:], exp_sum[:]))
            link(nc.vector.tensor_tensor(comb1[:], p1[:], count1[:, :, 0:EXPERTS1], ALU.mult))
            link(nc.vector.tensor_tensor(comb1[:], comb1[:], exp_rec[:].unsqueeze(2).to_broadcast([P, TILES, EXPERTS1]),
                                         ALU.mult))

            with dve.Fori(0, IN_SLABS // SLOTS) as i:
                for j in range(SLOTS):
                    for v in range(2):
                        unit = (2 * SLOTS) * i + (2 * j + v)
                        gated(PAIRS + unit, (PAIRS + v) % 2, False,
                              dest=(hid_hi[:, bass.ds(unit * TOKENS, TOKENS)], hid_lo[:, bass.ds(unit * TOKENS, TOKENS)]))
                    low(SLOTS * i + (IN_SLAB + SLOTS + j), (IN_SLAB + j) % SLOTS, SLAB_W)
            for s in (12 * SLOTS, 12 * SLOTS + 1):
                low(s, s % SLOTS, SLAB_W)
            for t, (ready, value) in enumerate(((shared_ready, 1), (slab_used, used_value(OUT_SLAB + 1)))):
                dve.wait_ge(ready, value)
                nc.vector.tensor_tensor(resid[:, t, :], resid[:, t, :], y[t][:], ALU.add).then_inc(added, 1)

            def add_expert(e, q, signal):
                for t in range(TILES):
                    if t == 0:
                        dve.wait_ge(expert_ready, e + 1)
                    else:
                        dve.wait_ge(slab_used, 2 * e + used_value(OUT_SLAB + 3))
                    dve.wait_ge(added, TILES * e + (t + 1))
                    nc.vector.scalar_tensor_tensor(resid[:, t, :], (gate_ps, up_ps)[q][t][:],
                                                   comb1[:, t, bass.ds(e, 1)], resid[:, t, :],
                                                   ALU.mult, ALU.add).then_inc(signal, 1)

            with dve.Fori(0, 3) as i:
                for q in range(2):
                    for v in range(2):
                        n = 2 + 2 * q + v
                        low(SLOTS * i + (12 * SLOTS + n), n % SLOTS, SLAB_W)
                    add_expert(2 * i + q, q, added)
            add_expert(EXPERTS1 - 2, 0, added)
            add_expert(EXPERTS1 - 1, 1, result_ready)

        @block.tensor
        def _(pe):
            def product(dest, left, right, start, stop):
                (lh, ll), (rh, rl) = left, right
                nc.tensor.matmul(dest, lh, rh, start=start, stop=False)
                nc.tensor.matmul(dest, lh, rl, start=False, stop=False)
                return nc.tensor.matmul(dest, ll, rh, start=False, stop=stop)

            def parts(a, index):
                return a[0][index], a[1][index]

            def transpose_tokens(source):
                for b in range(2):
                    for c in (2 * b, 2 * b + 1):
                        for t in range(TILES):
                            at = (c % 2) * TOKENS + t * P
                            last = nc.tensor.transpose(misc[b][:, at:at + P], source[:, t, c * P:(c + 1) * P], ident[:])
                    last.then_inc(transposed, 1)

            activ, agg = (zT_hi, zT_lo), (aggT_hi, aggT_lo)

            def dense(dest, left, s, ready):
                slot = s % SLOTS
                pe.wait_ge(hi_done, s + 1)
                low_wait(pe, s)
                for t, signal in enumerate((ready, slab_used)):
                    dense_tile(dest[t], left, slot, t, signal)

            def dense_tile(dest, left, slot, t, signal):
                for c in range(CHUNKS):
                    last = product(dest[:], parts(left, (slice(None), c, slice(t * P, (t + 1) * P))),
                                   (w_hi[slot][:, c * FEATURES:(c + 1) * FEATURES],
                                    w_lo[slot][:, c * FEATURES:(c + 1) * FEATURES]), c == 0, c == CHUNKS - 1)
                last.then_inc(signal, 1)

            def gate_and_up(slot, offset, q):
                for k, dest in enumerate((gate_ps[q], up_ps[q])):
                    for c in range(CHUNKS):
                        at = offset + (k * CHUNKS + c) * P
                        last = product(dest[:, 0:TOKENS], (w_hi[slot][:, at:at + P], w_lo[slot][:, at:at + P]),
                                       parts(activ, (slice(None), c, slice(None))), c == 0, c == CHUNKS - 1)
                last.then_inc(up_ready, 1)
                return last

            def count_column(col, j, start, stop):
                pe.wait_ge(hot_ready, col + 1)
                for t in range(TILES):
                    last = nc.tensor.matmul(gate_ps[t][:, 0:TOKENS], hot_src[:, j, t * P:(t + 1) * P],
                                            hot_dst[:, j, :], start=start, stop=stop)
                last.then_inc(hot_used, 1)

            for j in range(BLOCK):
                count_column(j, j, j == 0, False)
            pe.wait_ge(pool_const, 2)
            pe.wait_ge(z_ready, TILES)
            transpose_tokens(z)
            with pe.Fori(0, BLOCKS - 2) as i:
                for j in range(BLOCK):
                    count_column(BLOCK * i + (BLOCK + j), j, False, False)
            for j in range(BLOCK):
                count_column(BLOCK * (BLOCKS - 1) + j, j, False, j == BLOCK - 1)
            for t in range(TILES):
                pe.wait_ge(count_copied, TILES)
                for s in range(TILES):
                    last = nc.tensor.transpose(up_ps[t][:, s * P:(s + 1) * P], count_t[:, s, t * P:(t + 1) * P], ident[:])
                last.then_inc(count_flipped, 1)
            pe.wait_ge(zT_hi_done, 2)
            pe.wait_ge(zT_lo_done, 2)
            dense(y, activ, GCN_SLAB, u_ps_ready)
            pe.wait_ge(u_ready, TILES)
            pe.wait_ge(adj_ready, TILES)
            for t in range(TILES):
                for s in range(TILES):
                    last = nc.tensor.matmul(gate_ps[t][:], adj[:, s, t * P:(t + 1) * P], u[:, s, :],
                                            start=s == 0, stop=s == TILES - 1)
                last.then_inc(gcn_ready, 1)
            pe.wait_ge(z_ready, 2 * TILES)
            transpose_tokens(z)
            pe.wait_ge(zT_hi_done, 4)
            pe.wait_ge(zT_lo_done, 4)
            pe.wait_ge(gates_hi_done, 1)
            pe.wait_ge(gates_lo_done, 1)

            def router(dest, first, count):
                for t in range(TILES):
                    for c in range(CHUNKS):
                        at = first + c * count
                        last = product(dest[:, t * count:(t + 1) * count],
                                       parts(activ, (slice(None), c, slice(t * P, (t + 1) * P))),
                                       (gates_hi[:, at:at + count], gates_lo[:, at:at + count]), c == 0, c == CHUNKS - 1)
                last.then_inc(logits_ready, 1)

            router(misc[1], 0, EXPERTS)

            def pair_in(p, slot, q, at=None):
                s = p + PAIR_SLAB
                pe.wait_ge(hi_done, s + 1)
                low_wait(pe, s, first=at)
                return gate_and_up(slot, 0, q)

            def pair_spread(p, q):
                nc.tensor.matmul(misc[q][:, 0:TOKENS], pair_sel[:], comb_rows[:, bass.ds((p - 1) * TOKENS, TOKENS)],
                                 start=True, stop=True).then_inc(spread, 1)

            def pair_out(p, slot, q, start=False, stop=False):
                pe.wait_ge(g_lo_done, p + 1)
                for t in range(TILES):
                    last = product(y[t][:], (g_hi[q][:, t * P:(t + 1) * P], g_lo[q][:, t * P:(t + 1) * P]),
                                   (w_hi[slot][:, 2 * FEATURES:PAIR_W], w_lo[slot][:, 2 * FEATURES:PAIR_W]), start, stop)
                last.then_inc(slab_used, 1)
                return last

            pair_in(0, 1, 0)
            pair_in(1, 2, 1)
            pe.wait_ge(comb_hi_done, 1)
            pe.wait_ge(comb_lo_done, 1)
            for t in range(TILES):
                last = nc.tensor.transpose(misc[0][:, t * P:(t + 1) * P],
                                           comb_parts[:, t, :, :].rearrange("p a e -> p (a e)").bitcast(F32), ident[:])
            last.then_inc(combT_ps, 1)
            pair_out(0, 1, 0, start=True)
            pe.wait_ge(rows_in, 64)
            pe.wait_ge(pair_sel_done, 1)
            pair_spread(1, 1)
            pair_in(2, 3, 0)
            pair_spread(2, 0)
            pair_out(1, 2, 1)
            with pe.Fori(0, LOOP_ROUNDS) as i:
                for j in range(SLOTS):
                    p = SLOTS * i + (LOOP_FIRST + j)
                    slot = (LOOP_FIRST + j + PAIR_SLAB) % SLOTS
                    pair_in(p + 1, (slot + 1) % SLOTS, (j + 1) % 2, at=SLOTS)
                    pair_spread(p + 1, (j + 1) % 2)
                    pair_out(p, slot, j % 2)
            for p in range(LOOP_END, PAIRS):
                if p + 1 < PAIRS:
                    pair_in(p + 1, (p + 2) % SLOTS, (p + 1) % 2)
                    pair_spread(p + 1, (p + 1) % 2)
                pair_out(p, (p + 1) % SLOTS, p % 2, stop=p == PAIRS - 1)

            pe.wait_ge(z_ready, 3 * TILES)
            transpose_tokens(z)
            for b in range(2):
                for c in (2 * b, 2 * b + 1):
                    for s in range(TILES):
                        at = (c % 2) * TOKENS
                        last = nc.tensor.matmul(gate_ps[b][:, at:at + TOKENS], z[:, s, c * P:(c + 1) * P],
                                                count_t[:, s, :], start=s == 0, stop=s == TILES - 1)
                last.then_inc(agg_ready, 1)
            pe.wait_ge(zT_lo_done, 6)
            dense(up_ps, activ, SAGE_R_SLAB, sage_ready)
            pe.wait_ge(zT_lo_done, 8)
            dense(y, agg, SAGE_L_SLAB, sage_ready)

            pe.wait_ge(z_ready, 5 * TILES)
            transpose_tokens(z1)
            pe.wait_ge(zT_lo_done, 10)
            router(misc[0], CHUNKS * EXPERTS, GATES1)

            with pe.Fori(0, IN_SLABS // SLOTS) as i:
                for j in range(SLOTS):
                    s = SLOTS * i + (IN_SLAB + j)
                    pe.wait_ge(hi_done, s + 1)
                    if j == 0:
                        pe.wait_ge(dve_lo_done, IN_SLAB - SLOTS + 1 + i)
                    else:
                        pe.wait_ge(pool_lo_done, SLOTS + j)
                        pe.wait_ge(dve_lo_done, (j + 1) * i + (IN_SLAB - SLOTS + 1))
                    for v in range(2):
                        k = (2 * SLOTS) * i + (PAIRS + 2 * j + v)
                        pe.wait_ge(g_lo_done, k - 1)
                        gate_and_up((IN_SLAB + j) % SLOTS, v * UNIT_W, (PAIRS + v) % 2)

            pe.wait_ge(count1_ready, 1)
            for t in range(TILES):
                last = nc.tensor.transpose(misc[1][:, t * P:(t + 1) * P], count1[:, t, :], ident[:])
            last.then_inc(count1T_ps, 1)

            def hidden(unit, t):
                at = unit * TOKENS + t * P
                return hid_hi[:, at:at + P], hid_lo[:, at:at + P]

            def out_product(dest, first_unit, slot, half, t, start, stop):
                for c in range(CHUNKS):
                    last = product(dest[t][:], hidden(first_unit + half * CHUNKS + c, t),
                                   (w_hi[slot][:, c * FEATURES:(c + 1) * FEATURES],
                                    w_lo[slot][:, c * FEATURES:(c + 1) * FEATURES]),
                                   start and c == 0, stop and c == CHUNKS - 1)
                return last

            pe.wait_ge(count1T_ready, 1)
            pe.wait_ge(g_lo_done, PAIRS + UNITS)
            for t in range(TILES):
                nc.tensor.matmul(y[t][:], count1T[:, t * P:(t + 1) * P], out_bias[:], start=True, stop=False)

            def out_products(first_unit, dest, s, slot, at, ready, opened):
                for half in range(2):
                    pe.wait_ge(hi_done, s + half + 1)
                    low_wait(pe, s + half, first=at + half)
                    for t in range(TILES):
                        last = out_product(dest, first_unit, slot + half, half, t, not opened and half == 0, half == 1)
                        if half == 1 and t == 0:
                            last.then_inc(ready, 1)
                    last.then_inc(slab_used, 1)

            out_products(0, y, OUT_SLAB, 0, OUT_SLAB, shared_ready, True)
            for e in range(2):
                s = OUT_SLAB + 2 + 2 * e
                out_products(HIDDEN_CHUNKS, (gate_ps, up_ps)[e], s, s % SLOTS, s, expert_ready, False)
            with pe.Fori(0, 3) as i:
                for q in range(2):
                    pe.wait_ge(added, 4 * i + (4 + 2 * q))
                    s = OUT_SLAB + 2 + 2 * (2 + q)
                    out_products(HIDDEN_CHUNKS, (gate_ps, up_ps)[q], SLOTS * i + s, s % SLOTS, s, expert_ready, False)


_OUT = ((TOKENS, FEATURES), "float32")


def _slabs(**a):
    import numpy as np

    def chunks(w):
        k, n = w.shape
        return w.reshape(k // P, P, n).transpose(1, 0, 2).reshape(P, -1)

    def pair_in(w):
        return w.reshape(PAIRS, 2, CHUNKS, P, 64).transpose(0, 3, 2, 1, 4).reshape(PAIRS, P, -1)

    def units(w):
        return w.reshape(2, HIDDEN_CHUNKS, P, CHUNKS, P).transpose(1, 4, 0, 3, 2).reshape(HIDDEN_CHUNKS, P, -1)

    def outs(w):
        e = w.shape[0]
        return w.transpose(0, 2, 1).reshape(e, 2, CHUNKS, P, FEATURES).transpose(0, 1, 3, 2, 4).reshape(2 * e, P, -1)

    u = np.concatenate([units(a["L1_ffn_shared_in_w"]), units(a["L1_ffn_expert_in_w"])])
    return {
        "x": a["x"], "src": a["src"], "dst": a["dst"],
        "gcn_w": chunks(a["L0_gnn_weight"]), "gcn_b": a["L0_gnn_bias"],
        "pairs": np.concatenate([pair_in(a["L0_ffn_w1"]), pair_in(a["L0_ffn_w3"]),
                                 a["L0_ffn_w2"].reshape(PAIRS, P, FEATURES)], axis=2),
        "gates": np.concatenate([chunks(a["L0_ffn_g_w"].T),
                                 chunks(np.concatenate([a["L1_ffn_expert_gate_w"], a["L1_ffn_group_gate_w"]]).T)], axis=1),
        "gate_bias": a["L0_ffn_gate_bias"],
        "sage_r": chunks(a["L1_gnn_W_r"]), "sage_l": chunks(a["L1_gnn_W_l"]), "sage_b": a["L1_gnn_b"],
        "ln_affine": np.stack([a["L1_ffn_ln_scale"].reshape(CHUNKS, P).T, a["L1_ffn_ln_bias"].reshape(CHUNKS, P).T]),
        "units": u.reshape(IN_SLABS, 2, P, UNIT_W).transpose(0, 2, 1, 3).reshape(IN_SLABS, P, SLAB_W),
        "outs": np.concatenate([outs(a["L1_ffn_shared_out_w"][None]), outs(a["L1_ffn_expert_out_weight"])]),
        "out_bias": np.concatenate([a["L1_ffn_expert_out_bias"], a["L1_ffn_shared_out_b"][None]]),
        "gate1_bias": np.concatenate([a["L1_ffn_expert_bias"], a["L1_ffn_group_bias"]]),
    }


def kernel(**inputs):
    import concourse.bacc as bacc
    import numpy as np
    from concourse.bass_utils import run_bass_kernel_spmd

    nc = bacc.Bacc("TRN2", target_bir_lowering=False, num_devices=1)
    arrays, args = {}, []
    for name, a in _slabs(**{k: np.asarray(v) for k, v in inputs.items()}).items():
        a = np.ascontiguousarray(a)
        arrays[f"in_{name}"] = a
        args.append(nc.dram_tensor(f"in_{name}", a.shape, mybir.dt.from_np(a.dtype), kind="ExternalInput").ap())
    args.append(nc.dram_tensor("out", _OUT[0], mybir.dt.from_np(np.dtype(_OUT[1])), kind="ExternalOutput").ap())
    build(nc, *args)
    return run_bass_kernel_spmd(nc, [arrays], core_ids=[0]).results[0]["out"]
```

```python
from contextlib import ExitStack

import concourse.bass as bass
from concourse import mybir

F32 = mybir.dt.float32
F32R = mybir.dt.float32r
BF16 = mybir.dt.bfloat16
I32 = mybir.dt.int32
U32 = mybir.dt.uint32
ALU = mybir.AluOpType
ACT = mybir.ActivationFunctionType
AX = mybir.AxisListType

P = 128
TOKENS, FEATURES, EDGES = 256, 512, 8192
TILES = TOKENS // P
CHUNKS = FEATURES // P
EDGE_COLS = EDGES // P
LN_EPS = 1e-5

EXPERTS, TOP_K, PAIRS, ROUTED_PAIRS = 64, 6, 33, 32
UNITS, HIDDEN_CHUNKS, EXPERTS1, GROUPS = 16, 8, 8, 2
GATES1 = EXPERTS1 + GROUPS

SLOTS = 4
SLAB_W = 2048
PAIR_W = 1536
UNIT_W = 1024
GCN_SLAB = 0
PAIR_SLAB = 1
SAGE_R_SLAB = PAIR_SLAB + PAIRS
SAGE_L_SLAB = SAGE_R_SLAB + 1
IN_SLAB = SAGE_L_SLAB + 1
IN_SLABS = UNITS // 2
OUT_SLAB = IN_SLAB + IN_SLABS
OUT_SLABS = 2 + 2 * EXPERTS1
SLABS = OUT_SLAB + OUT_SLABS

BLOCK = 8
BLOCKS = EDGE_COLS // BLOCK
LOOP_FIRST, LOOP_ROUNDS = 2, 7
LOOP_END = LOOP_FIRST + LOOP_ROUNDS * SLOTS

BIG = 1e30


def pool_makes_low(s):
    return s < SLOTS or IN_SLAB < s < IN_SLAB + SLOTS - 1


def slab_width(s):
    return PAIR_W if PAIR_SLAB <= s < SAGE_R_SLAB else SLAB_W


def used_value(s):
    return s + 1 if s < IN_SLAB else s + 1 - IN_SLABS


def build(nc, x_in, src_in, dst_in, gcn_w_in, gcn_b_in, pairs_in, gates_in, gate_bias_in,
          sage_r_in, sage_l_in, sage_b_in, ln_scale_in, ln_bias_in, units_in, outs_in, out_bias_in,
          gate1_bias_in, out):
    with ExitStack() as ctx:
        def sb(name, shape, dt=F32):
            return ctx.enter_context(nc.sbuf_tensor(name, shape, dt))

        def sem(name):
            return ctx.enter_context(nc.semaphore(name))

        raw = [sb(f"raw{i}", [P, SLAB_W]) for i in range(SLOTS)]
        w_hi = [sb(f"w_hi{i}", [P, SLAB_W], F32R) for i in range(SLOTS)]
        w_lo = [sb(f"w_lo{i}", [P, SLAB_W], F32R) for i in range(SLOTS)]
        gates = sb("gates", [P, CHUNKS, P])
        gates_hi = sb("gates_hi", [P, CHUNKS, P], F32R)
        gates_lo = sb("gates_lo", [P, CHUNKS, P], F32R)
        gcn_b = sb("gcn_b", [P, FEATURES])
        sage_b = sb("sage_b", [P, FEATURES])
        gate_bias = sb("gate_bias", [P, EXPERTS])
        gate1_bias = sb("gate1_bias", [P, GATES1])
        out_bias = sb("out_bias", [EXPERTS1 + 1, FEATURES])
        ident = sb("ident", [P, P])
        diag = sb("diag", [P, TILES, TOKENS])
        iota_i = sb("iota_i", [P, TOKENS], I32)
        iota_b = sb("iota_b", [P, TOKENS], BF16)
        iota_f = sb("iota_f", [P, EXPERTS])
        minus_half = sb("minus_half", [P, TILES])
        pair_sel_f = sb("pair_sel_f", [4, P])
        pair_sel = sb("pair_sel", [4, P], F32R)
        edges_i = sb("edges_i", [P, 2, EDGE_COLS], I32)
        edges_f = sb("edges_f", [P, 2, EDGE_COLS])
        hot_src = sb("hot_src", [P, BLOCK, TOKENS], BF16)
        hot_dst = sb("hot_dst", [P, BLOCK, TOKENS], BF16)
        count_t = sb("count_t", [P, TILES, TOKENS])
        both_ways = sb("both_ways", [P, TILES, TOKENS])
        ln_scale, ln_bias = (a[:].rearrange("p t n -> p (t n)") for a in (diag, both_ways))
        adj = sb("adj", [P, TILES, TOKENS], F32R)
        deg = sb("deg", [P, TILES])
        dinv = sb("dinv", [P, TILES])
        in_deg = sb("in_deg", [P, TILES])
        rdeg = sb("rdeg", [P, TILES])
        x = sb("x", [P, TILES, FEATURES])
        resid = sb("resid", [P, TILES, FEATURES])
        z = sb("z", [P, TILES, FEATURES])
        zT_hi = sb("zT_hi", [P, CHUNKS, TOKENS], F32R)
        zT_lo = sb("zT_lo", [P, CHUNKS, TOKENS], F32R)
        aggT_hi = sb("aggT_hi", [P, CHUNKS, TOKENS], F32R)
        aggT_lo = sb("aggT_lo", [P, CHUNKS, TOKENS], F32R)
        u_hi, u_lo = (a[:].rearrange("p c n -> p (c n)").rearrange("p (t f) -> p t f", t=TILES)
                      for a in (aggT_hi, aggT_lo))
        logitsT = sb("logitsT", [P, TOKENS])
        stats = sb("stats", [P, TILES, 6])
        mean_var = sb("mean_var", [P, TILES, 2])
        var_eps = sb("var_eps", [P, TILES])
        rstd = sb("rstd", [P, TILES])
        top = sb("top", [P, TILES, 8])
        top_i = sb("top_i", [P, TILES, 8], U32)
        top_f = sb("top_f", [P, TILES, 8])
        neg_max = sb("neg_max", [P, TILES])
        exp_sum = sb("exp_sum", [P, TILES])
        exp_rec = sb("exp_rec", [P, TILES])
        probs = sb("probs", [P, TILES, EXPERTS])
        picked = sb("picked", [P, TILES, EXPERTS])
        replaced = sb("replaced", [P, TILES, EXPERTS])
        not_top = sb("not_top", [P, TILES, EXPERTS])
        comb = sb("comb", [P, TILES, EXPERTS])
        comb_parts = sb("comb_parts", [P, TILES, 2, EXPERTS], F32R)
        combT = sb("combT", [P, TOKENS], F32R)
        logits1 = sb("logits1", [P, TILES, GATES1])
        group_on = sb("group_on", [P, TILES, GROUPS])
        group_pen = sb("group_pen", [P, TILES, GROUPS])
        e1 = sb("e1", [P, TILES, EXPERTS1])
        p1 = sb("p1", [P, TILES, EXPERTS1])
        hits1 = sb("hits1", [P, TILES, 2, EXPERTS1])
        count1 = sb("count1", [P, TILES, P])
        count1T = sb("count1T", [EXPERTS1 + 1, TOKENS])
        comb1 = sb("comb1", [P, TILES, EXPERTS1])
        silu = [sb(f"silu{i}", [P, TOKENS]) for i in range(2)]
        glu = [sb(f"glu{i}", [P, TOKENS]) for i in range(2)]
        g = [sb(f"g{i}", [P, TOKENS]) for i in range(2)]
        g_hi = [sb(f"g_hi{i}", [P, TOKENS], F32R) for i in range(2)]
        g_lo = [sb(f"g_lo{i}", [P, TOKENS], F32R) for i in range(2)]
        hid = sb("hid", [P, 2 * UNITS * TOKENS], F32R)
        hid_hi, hid_lo = hid[:, 0:UNITS * TOKENS], hid[:, UNITS * TOKENS:]
        comb_rows = hid[0:4, 0:ROUTED_PAIRS * TOKENS]

        bank = [ctx.enter_context(nc.psum_tensor(f"bank{i}", [P, 512], F32)) for i in range(8)]
        y = bank[0:2]
        gate_ps = bank[2:4]
        up_ps = bank[4:6]
        misc = bank[6:8]
        pair_banks = [(gate_ps[0], up_ps[0]), (gate_ps[1], up_ps[1]), (y[0], y[1]), (misc[0], misc[1])]

        edges_in, x_in_s, consts_in = sem("edges_in"), sem("x_in"), sem("consts_in")
        raw_in = [sem(f"raw_in{i}") for i in range(SLOTS)]
        hi_done, dve_lo_done, pool_lo_done = sem("hi_done"), sem("dve_lo_done"), sem("pool_lo_done")
        slab_used = sem("slab_used")
        gates_hi_done, gates_lo_done = sem("gates_hi_done"), sem("gates_lo_done")
        pool_const, pool_chain, pad_done = sem("pool_const"), sem("pool_chain"), sem("pad_done")
        pair_sel_done = sem("pair_sel_done")
        bias_added = sem("bias_added")
        var_ready, rstd_ready, z_ready = sem("var_ready"), sem("rstd_ready"), sem("z_ready")
        transposed, zT_hi_done, zT_lo_done = sem("transposed"), sem("zT_hi_done"), sem("zT_lo_done")
        affine_in, scaled = sem("affine_in"), sem("scaled")
        hot_ready, hot_used = sem("hot_ready"), sem("hot_used")
        count_copied, count_flipped = sem("count_copied"), sem("count_flipped")
        deg_ready, dinv_ready = sem("deg_ready"), sem("dinv_ready")
        u_hi_done, u_lo_done = sem("u_hi_done"), sem("u_lo_done")
        u_ps_ready, gcn_ready = sem("u_ps_ready"), sem("gcn_ready")
        logitsT_ready, logitsT_copied = sem("logitsT_ready"), sem("logitsT_copied")
        logits_ready, max_ready, exp_ready = sem("logits_ready"), sem("max_ready"), sem("exp_ready")
        comb_ready, comb_hi_done, comb_lo_done = sem("comb_ready"), sem("comb_hi_done"), sem("comb_lo_done")
        combT_ps, combT_ready, rows_in = sem("combT_ps"), sem("combT_ready"), sem("rows_in")
        up_ready, silu_done, glu_done = sem("up_ready"), sem("silu_done"), sem("glu_done")
        spread, g_done, g_hi_done, g_lo_done = sem("spread"), sem("g_done"), sem("g_hi_done"), sem("g_lo_done")
        agg_ready = sem("agg_ready")
        sage_ready = sem("sage_ready")
        logits1_ready = sem("logits1_ready")
        exp1_in, exp1_done = sem("exp1_in"), sem("exp1_done")
        count1_ready, count1T_ps, count1T_ready = sem("count1_ready"), sem("count1T_ps"), sem("count1T_ready")
        shared_ready, expert_ready, added = sem("shared_ready"), sem("expert_ready"), sem("added")
        dve_chain = sem("dve_chain")
        result_ready, stored = sem("result_ready"), sem("stored")

        block = ctx.enter_context(nc.Block())

        def tile_of(a, t):
            return a[:, :, t * P:(t + 1) * P]

        def low_wait(eng, s, first=None):
            at = s if first is None else first
            if pool_makes_low(at):
                eng.wait_ge(pool_lo_done, s + 1 if at < SLOTS else s - IN_SLAB + SLOTS)
            elif at <= IN_SLAB:
                eng.wait_ge(dve_lo_done, s - SLOTS + 1)
            else:
                eng.wait_ge(dve_lo_done, s - 2 * SLOTS + 3)

        @block.sync
        def _(sp):
            def load(slot, source, width):
                sp.dma_start(raw[slot][:, 0:width], source).then_inc(raw_in[slot], 16)

            sp.dma_start(edges_i[:, 0, :], src_in.rearrange("(p j) -> p j", p=P)).then_inc(edges_in, 16)
            sp.dma_start(edges_i[:, 1, :], dst_in.rearrange("(p j) -> p j", p=P)).then_inc(edges_in, 16)
            sp.dma_start(x[:], x_in.rearrange("(t p) f -> p t f", p=P)).then_inc(x_in_s, 16)
            load(0, gcn_w_in, SLAB_W)
            for s in range(PAIR_SLAB, 2 * SLOTS):
                if s >= SLOTS:
                    low_wait(sp, s - SLOTS)
                load(s % SLOTS, pairs_in[s - PAIR_SLAB], PAIR_W)
            with sp.Fori(0, 6) as i:
                for j in range(SLOTS):
                    s = 2 * SLOTS + SLOTS * i + j
                    low_wait(sp, s - SLOTS, first=SLOTS + j)
                    load(j, pairs_in[bass.ds(s - PAIR_SLAB, 1), :, :].rearrange("a p w -> p (a w)"), PAIR_W)
            sp.wait_ge(deg_ready, TILES)
            sp.dma_start(ln_scale, ln_scale_in.partition_broadcast(P)).then_inc(affine_in, 16)
            sp.dma_start(ln_bias, ln_bias_in.partition_broadcast(P)).then_inc(affine_in, 16)
            for s in range(8 * SLOTS, 12 * SLOTS):
                low_wait(sp, s - SLOTS)
                if s < SAGE_R_SLAB:
                    load(s % SLOTS, pairs_in[s - PAIR_SLAB], PAIR_W)
                elif s == SAGE_R_SLAB:
                    load(s % SLOTS, sage_r_in, SLAB_W)
                elif s == SAGE_L_SLAB:
                    load(s % SLOTS, sage_l_in, SLAB_W)
                elif s < OUT_SLAB:
                    load(s % SLOTS, units_in[s - IN_SLAB], SLAB_W)
                else:
                    load(s % SLOTS, outs_in[s - OUT_SLAB], SLAB_W)
            with sp.Fori(0, 3) as i:
                for j in range(SLOTS):
                    s = 12 * SLOTS + SLOTS * i + j
                    low_wait(sp, s - SLOTS, first=11 * SLOTS + j)
                    load(j, outs_in[bass.ds(s - OUT_SLAB, 1), :, :].rearrange("a p w -> p (a w)"), SLAB_W)
            for s in range(15 * SLOTS, SLABS):
                low_wait(sp, s - SLOTS)
                load(s % SLOTS, outs_in[s - OUT_SLAB], SLAB_W)
            for t in range(TILES):
                sp.wait_ge(result_ready, t + 1)
                sp.dma_start(out[t * P:(t + 1) * P, :], resid[:, t, :]).then_inc(stored, 16)
            sp.wait_ge(stored, 16 * TILES)

        @block.gpsimd
        def _(pool):
            chain = [0]

            def link(ins):
                chain[0] += 1
                ins.then_inc(pool_chain, 1)
                pool.wait_ge(pool_chain, chain[0])

            link(nc.gpsimd.iota(iota_i[:], [[1, TOKENS]], base=0, channel_multiplier=0))
            nc.gpsimd.tensor_copy(iota_b[:], iota_i[:]).then_inc(pool_const, 1)
            link(nc.gpsimd.memset(ident[:], 0.0))
            nc.gpsimd.affine_select(out=ident[:], in_=ident[:], compare_op=ALU.not_equal, fill=1.0, base=0,
                                    pattern=[[-1, P]], channel_multiplier=1).then_inc(pool_const, 1)
            link(nc.gpsimd.memset(minus_half[:], -0.5))
            nc.gpsimd.memset(gates[:], 0.0).then_inc(pad_done, 1)

            def inverse_roots(n):
                for t in range(TILES):
                    pool.wait_ge(var_ready, TILES * (n - 1) + t + 1)
                    nc.gpsimd.tensor_tensor(rstd[:, t:t + 1], var_eps[:, t:t + 1], minus_half[:, t:t + 1],
                                            ALU.pow).then_inc(rstd_ready, 1)

            inverse_roots(1)
            nc.gpsimd.tensor_copy(iota_f[:], iota_i[:, 0:EXPERTS]).then_inc(pool_const, 1)
            link(nc.gpsimd.memset(diag[:], 0.0))
            nc.gpsimd.affine_select(out=diag[:], in_=diag[:], compare_op=ALU.not_equal, fill=1.0, base=0,
                                    pattern=[[P, TILES], [-1, TOKENS]], channel_multiplier=1).then_inc(pool_const, 1)
            link(nc.gpsimd.memset(pair_sel_f[:], 1.0))
            link(nc.gpsimd.affine_select(out=pair_sel_f[:, 0:64], in_=pair_sel_f[:, 0:64], compare_op=ALU.is_ge,
                                         fill=0.0, base=1, pattern=[[0, 64]], channel_multiplier=-1))
            link(nc.gpsimd.affine_select(out=pair_sel_f[:, 64:P], in_=pair_sel_f[:, 64:P], compare_op=ALU.is_ge,
                                         fill=0.0, base=-2, pattern=[[0, 64]], channel_multiplier=1))
            nc.gpsimd.tensor_copy(pair_sel[:], pair_sel_f[:]).then_inc(pair_sel_done, 1)
            nc.gpsimd.memset(count1[:], 1.0).then_inc(pool_const, 1)

            def low(s, width):
                pool.wait_ge(hi_done, s + 1)
                nc.gpsimd.tensor_tensor(w_lo[s % SLOTS][:, 0:width], raw[s % SLOTS][:, 0:width],
                                        w_hi[s % SLOTS][:, 0:width].bitcast(F32), ALU.subtract).then_inc(pool_lo_done, 1)

            low(0, SLAB_W)
            pool.wait_ge(x_in_s, 16)
            pool.wait_ge(consts_in, 16 * 6)
            for t in range(TILES):
                nc.gpsimd.tensor_tensor(resid[:, t, :], x[:, t, :], gcn_b[:], ALU.add).then_inc(bias_added, 1)
            pool.wait_ge(gates_hi_done, 1)
            nc.gpsimd.tensor_tensor(gates_lo[:], gates[:], gates_hi[:].bitcast(F32), ALU.subtract).then_inc(gates_lo_done, 1)
            for s in range(PAIR_SLAB, SLOTS):
                low(s, PAIR_W)
            pool.wait_ge(deg_ready, TILES)
            nc.gpsimd.tensor_tensor(dinv[:], deg[:], minus_half[:], ALU.pow).then_inc(dinv_ready, 1)

            inverse_roots(2)
            inverse_roots(3)
            for t in range(TILES):
                nc.gpsimd.tensor_tensor(x[:, t, :], resid[:, t, :], sage_b[:], ALU.add).then_inc(bias_added, 1)
            low(IN_SLAB + 1, SLAB_W)
            inverse_roots(4)
            low(IN_SLAB + 2, SLAB_W)

        @block.scalar
        def _(act):
            act.dma_start(gcn_b[:], gcn_b_in.partition_broadcast(P)).then_inc(consts_in, 16)
            act.wait_ge(pad_done, 1)
            act.dma_start(gates[:, :, 0:EXPERTS + GATES1], gates_in).then_inc(consts_in, 16)
            act.dma_start(gate_bias[:], gate_bias_in.partition_broadcast(P)).then_inc(consts_in, 16)
            act.dma_start(sage_b[:], sage_b_in.partition_broadcast(P)).then_inc(consts_in, 16)
            act.dma_start(gate1_bias[:], gate1_bias_in.partition_broadcast(P)).then_inc(consts_in, 16)
            act.dma_start(out_bias[:], out_bias_in).then_inc(consts_in, 16)

            def high(s, slot, width, used=None):
                act.wait_ge(raw_in[slot], (s - slot) * (16 // SLOTS) + 16)
                if used is not None:
                    act.wait_ge(slab_used, used)
                nc.scalar.activation(w_hi[slot][:, 0:width], raw[slot][:, 0:width], ACT.Copy).then_inc(hi_done, 1)

            def split_transposed(n):
                for t in range(TILES):
                    act.wait_ge(transposed, TILES * n + t + 1)
                    nc.scalar.activation(tile_of(zT_hi, t), misc[t][:].rearrange("p (c n) -> p c n", c=CHUNKS),
                                         ACT.Copy).then_inc(zT_hi_done, 1)

            def copy_logits(n):
                act.wait_ge(logitsT_ready, n)
                nc.scalar.activation(logitsT[:], misc[1][:, 0:TOKENS], ACT.Copy).then_inc(logitsT_copied, 1)

            high(0, 0, SLAB_W)
            split_transposed(0)
            act.wait_ge(consts_in, 16 * 6)
            nc.scalar.activation(gates_hi[:], gates[:], ACT.Copy).then_inc(gates_hi_done, 1)
            for s in range(PAIR_SLAB, SLOTS):
                high(s, s, PAIR_W)
            for t in range(TILES):
                act.wait_ge(hot_used, EDGE_COLS)
                nc.scalar.activation(count_t[:, t, :], gate_ps[t][:, 0:TOKENS], ACT.Copy).then_inc(count_copied, 1)
            for t, ready in enumerate((u_ps_ready, slab_used)):
                act.wait_ge(ready, 1)
                act.wait_ge(dinv_ready, 1)
                nc.scalar.activation(u_hi[:, t, :], y[t][:], ACT.Copy, scale=dinv[:, t:t + 1]).then_inc(u_hi_done, 1)
            split_transposed(1)
            copy_logits(1)

            def act_silu(k, q, source=None):
                act.wait_ge(up_ready, k + 1)
                nc.scalar.activation(silu[q][:], (source or gate_ps[q])[:, 0:TOKENS], ACT.Silu).then_inc(silu_done, 1)

            def act_g_high(k, q, dest=None):
                act.wait_ge(g_done, k + 1)
                nc.scalar.activation(g_hi[q][:] if dest is None else dest, g[q][:], ACT.Copy).then_inc(g_hi_done, 1)

            for t in range(TILES):
                act.wait_ge(max_ready, 1)
                nc.scalar.activation(probs[:, t, :], misc[0][:, t * P:t * P + EXPERTS], ACT.Exp,
                                     bias=neg_max[:, t:t + 1], accum_out=exp_sum[:, t:t + 1]).then_inc(exp_ready, 1)
            act_silu(0, 0)
            act.wait_ge(comb_ready, TILES)
            nc.scalar.activation(comb_parts[:, :, 0, :], comb[:], ACT.Copy).then_inc(comb_hi_done, 1)
            act_g_high(0, 0)
            act.wait_ge(combT_ps, 1)
            nc.scalar.activation(combT[:], misc[0][:, 0:TOKENS], ACT.Copy).then_inc(combT_ready, 1)
            act.wait_ge(combT_ready, 1)
            for k in range(2):
                for part in range(2):
                    first = part * EXPERTS + k
                    row = 2 * k + part
                    act.dma_start(comb_rows[row:row + 1, :].bitcast(F32).rearrange("r (a n) -> r a n", n=TOKENS),
                                  combT[first:part * EXPERTS + EXPERTS:2, :].bitcast(F32)).then_inc(rows_in, 16)
            high(4, 0, PAIR_W, used=1)
            act_silu(1, 1)
            act_g_high(1, 1)
            high(5, 1, PAIR_W, used=2)
            with act.Fori(0, LOOP_ROUNDS) as i:
                for j in range(SLOTS):
                    p = SLOTS * i + (LOOP_FIRST + j)
                    act_silu(p, j % 2)
                    act_g_high(p, j % 2)
                    high(p + 4, (LOOP_FIRST + j) % SLOTS, PAIR_W, used=p + 1)
            for p in range(LOOP_END, PAIRS):
                act_silu(p, p % 2)
                act_g_high(p, p % 2)
                high(p + 4, (p + 4) % SLOTS, slab_width(p + 4), used=p + 1)
            high(IN_SLAB + 1, (IN_SLAB + 1) % SLOTS, SLAB_W, used=used_value(IN_SLAB - 3))
            split_transposed(2)
            for b in range(2):
                act.wait_ge(agg_ready, b + 1)
                nc.scalar.activation(aggT_hi[:, 2 * b:2 * b + 2, :],
                                     gate_ps[b][:].rearrange("p (c n) -> p c n", c=2), ACT.Copy).then_inc(zT_hi_done, 1)
            for s in (IN_SLAB + 2, IN_SLAB + 3):
                high(s, s % SLOTS, SLAB_W, used=used_value(s - SLOTS))
            split_transposed(3)
            copy_logits(2)
            with act.Fori(0, IN_SLABS // SLOTS) as i:
                for j in range(SLOTS):
                    for v in range(2):
                        unit = (2 * SLOTS) * i + (2 * j + v)
                        act_silu(PAIRS + unit, (PAIRS + v) % 2, pair_banks[(2 * j + v) % 4][0])
                        act_g_high(PAIRS + unit, (PAIRS + v) % 2, hid_hi[:, bass.ds(unit * TOKENS, TOKENS)])
                    high(SLOTS * i + (IN_SLAB + SLOTS + j), (IN_SLAB + j) % SLOTS, SLAB_W)
            act.wait_ge(exp1_in, 1)
            nc.scalar.activation(p1[:], e1[:], ACT.Exp).then_inc(exp1_done, 1)
            high(12 * SLOTS, 0, SLAB_W, used=used_value(11 * SLOTS))
            act.wait_ge(count1T_ps, 1)
            nc.scalar.activation(count1T[:], misc[1][0:EXPERTS1 + 1, 0:TOKENS], ACT.Copy).then_inc(count1T_ready, 1)
            with act.Fori(0, 3) as i:
                for j in range(1, SLOTS + 1):
                    high(SLOTS * i + (12 * SLOTS + j), j % SLOTS, SLAB_W, used=SLOTS * i + used_value(11 * SLOTS + j))
            for s in range(15 * SLOTS + 1, SLABS):
                high(s, s % SLOTS, SLAB_W, used=used_value(s - SLOTS))

        @block.vector
        def _(dve):
            chain = [0]

            def link(ins):
                chain[0] += 1
                ins.then_inc(dve_chain, 1)
                dve.wait_ge(dve_chain, chain[0])

            def count(ins):
                chain[0] += 1
                ins.then_inc(dve_chain, 1)
                return chain[0]

            def done(value):
                dve.wait_ge(dve_chain, value)

            def norm_stats(source, t, factor=1.0, eps=LN_EPS):
                link(nc.vector.bn_stats(stats[:, t, :], source[:, t, :]))
                link(nc.vector.bn_aggr(mean_var[:, t, :], stats[:, t, :]))
                nc.vector.tensor_scalar(var_eps[:, t:t + 1], mean_var[:, t, 1:2], factor, eps, ALU.mult,
                                        ALU.add).then_inc(var_ready, 1)

            def norm_apply(source, t, n):
                dve.wait_ge(rstd_ready, TILES * (n - 1) + t + 1)
                nc.vector.tensor_scalar(z[:, t, :], source[:, t, :], mean_var[:, t, 0:1], rstd[:, t:t + 1],
                                        ALU.subtract, ALU.mult).then_inc(z_ready, 1)

            def low(s, slot, width):
                dve.wait_ge(hi_done, s + 1)
                nc.vector.tensor_tensor(w_lo[slot][:, 0:width], raw[slot][:, 0:width],
                                        w_hi[slot][:, 0:width].bitcast(F32), ALU.subtract).then_inc(dve_lo_done, 1)

            def low_transposed(n):
                for t in range(TILES):
                    dve.wait_ge(zT_hi_done, TILES * (n if n < 3 else n + 1) + t + 1)
                    nc.vector.tensor_tensor(tile_of(zT_lo, t), misc[t][:].rearrange("p (c n) -> p c n", c=CHUNKS),
                                            tile_of(zT_hi, t).bitcast(F32), ALU.subtract).then_inc(zT_lo_done, 1)

            dve.wait_ge(edges_in, 32)
            link(nc.vector.tensor_copy(edges_f[:], edges_i[:]))

            def hot_column(col, j):
                nc.vector.tensor_scalar(hot_src[:, j, :], iota_b[:], edges_f[:, 0, bass.ds(col, 1)], None, ALU.is_equal)
                nc.vector.tensor_scalar(hot_dst[:, j, :], iota_b[:], edges_f[:, 1, bass.ds(col, 1)], None,
                                        ALU.is_equal).then_inc(hot_ready, 1)

            dve.wait_ge(pool_const, 1)
            for j in range(BLOCK):
                hot_column(j, j)
            dve.wait_ge(x_in_s, 16)
            for t in range(TILES):
                norm_stats(x, t)
            for t in range(TILES):
                norm_apply(x, t, 1)
            with dve.Fori(0, BLOCKS - 1) as i:
                for j in range(BLOCK):
                    dve.wait_ge(hot_used, BLOCK * i + (j + 1))
                    hot_column(BLOCK * i + (BLOCK + j), j)
            low_transposed(0)
            dve.wait_ge(pool_const, 4)
            for t in range(TILES):
                dve.wait_ge(count_copied, t + 1)
                dve.wait_ge(count_flipped, t + 1)
                link(nc.vector.tensor_tensor(both_ways[:, t, :], up_ps[t][:, 0:TOKENS], count_t[:, t, :], ALU.add))
                nc.vector.scalar_tensor_tensor(adj[:, t, :], both_ways[:, t, :], 1.0, diag[:, t, :], ALU.min, ALU.add,
                                               accum_out=deg[:, t:t + 1]).then_inc(deg_ready, 1)
            for t in range(TILES):
                link(nc.vector.tensor_reduce(in_deg[:, t:t + 1], up_ps[t][:, 0:TOKENS], axis=AX.X, op=ALU.add))
            link(nc.vector.tensor_scalar(in_deg[:], in_deg[:], 1.0, None, ALU.max))
            link(nc.vector.reciprocal(rdeg[:], in_deg[:]))
            dve.wait_ge(dinv_ready, 1)
            for t in range(TILES):
                dve.wait_ge(u_hi_done, t + 1)
                nc.vector.scalar_tensor_tensor(u_lo[:, t, :], y[t][:], dinv[:, t:t + 1], u_hi[:, t, :].bitcast(F32),
                                               ALU.mult, ALU.subtract).then_inc(u_lo_done, 1)
            dve.wait_ge(bias_added, TILES)
            for t in range(TILES):
                dve.wait_ge(gcn_ready, t + 1)
                link(nc.vector.scalar_tensor_tensor(resid[:, t, :], gate_ps[t][:], dinv[:, t:t + 1], resid[:, t, :],
                                                    ALU.mult, ALU.add))
                norm_stats(resid, t)
                if t == 1:
                    norm_apply(resid, 0, 2)
            norm_apply(resid, 1, 2)
            low_transposed(1)

            dve.wait_ge(logits_ready, 1)
            scores = misc[0][:, 0:TILES * P].rearrange("p (t e) -> p t e", e=P)[:, :, 0:EXPERTS]
            link(nc.vector.tensor_reduce(neg_max[:], scores, axis=AX.X, op=ALU.max))
            nc.vector.tensor_scalar(neg_max[:], neg_max[:], -1.0, None, ALU.mult).then_inc(max_ready, 1)
            dve.wait_ge(exp_ready, TILES)
            link(nc.vector.reciprocal(exp_rec[:], exp_sum[:]))
            step = [count(nc.vector.scalar_tensor_tensor(picked[:, t, :], probs[:, t, :], exp_rec[:, t:t + 1],
                                                         gate_bias[:], ALU.mult, ALU.add)) for t in range(TILES)]
            after = []
            for t in range(TILES):
                done(step[t])
                after.append(count(nc.vector.max(top[:, t, :], picked[:, t, :])))
            step = after
            after = []
            for t in range(TILES):
                done(step[t])
                after.append(count(nc.vector.max_index(top_i[:, t, :], top[:, t, :], picked[:, t, :])))
            replaced_at = [count(nc.vector.match_replace(replaced[:, t, :], top[:, t, :], picked[:, t, :], -BIG))
                           for t in range(TILES)]
            done(after[1])
            cast = count(nc.vector.tensor_copy(top_f[:], top_i[:]))
            after = []
            for t in range(TILES):
                done(replaced_at[t])
                after.append(count(nc.vector.tensor_tensor(replaced[:, t, :], replaced[:, t, :], picked[:, t, :],
                                                           ALU.not_equal)))
            step = after
            done(cast)
            after = []
            for t in range(TILES):
                done(step[t])
                after.append(count(nc.vector.scalar_tensor_tensor(
                    not_top[:, t, :], iota_f[:], top_f[:, t, TOP_K:TOP_K + 1], replaced[:, t, :],
                    ALU.is_equal, ALU.subtract)))
            step = after
            after = []
            for t in range(TILES):
                done(step[t])
                after.append(count(nc.vector.scalar_tensor_tensor(
                    replaced[:, t, :], iota_f[:], top_f[:, t, TOP_K + 1:TOP_K + 2], not_top[:, t, :],
                    ALU.is_equal, ALU.add)))
            step = after
            link(nc.vector.tensor_scalar(exp_rec[:], exp_rec[:], -1.0, None, ALU.mult))
            for t in range(TILES):
                done(step[t])
                nc.vector.scalar_tensor_tensor(comb[:, t, :], probs[:, t, :], exp_rec[:, t:t + 1], replaced[:, t, :],
                                               ALU.mult, ALU.mult).then_inc(comb_ready, 1)
            dve.wait_ge(silu_done, 1)
            nc.vector.tensor_tensor(g[0][:], silu[0][:], up_ps[0][:, 0:TOKENS], ALU.mult).then_inc(g_done, 1)
            dve.wait_ge(comb_hi_done, 1)
            nc.vector.tensor_tensor(comb_parts[:, :, 1, :], comb[:], comb_parts[:, :, 0, :].bitcast(F32),
                                    ALU.subtract).then_inc(comb_lo_done, 1)
            dve.wait_ge(g_hi_done, 1)
            nc.vector.tensor_tensor(g_lo[0][:], g[0][:], g_hi[0][:].bitcast(F32), ALU.subtract).then_inc(g_lo_done, 1)

            def gated(k, q, weighted, dest=None, source=None):
                dve.wait_ge(silu_done, k + 1)
                if weighted:
                    nc.vector.tensor_tensor(glu[q][:], silu[q][:], up_ps[q][:, 0:TOKENS], ALU.mult).then_inc(glu_done, 1)
                    dve.wait_ge(spread, k)
                    dve.wait_ge(glu_done, k)
                    nc.vector.tensor_tensor(g[q][:], glu[q][:], misc[q][:, 0:TOKENS], ALU.mult).then_inc(g_done, 1)
                else:
                    nc.vector.tensor_tensor(g[q][:], silu[q][:], source[:, 0:TOKENS], ALU.mult).then_inc(g_done, 1)
                dve.wait_ge(g_hi_done, k + 1)
                hi, lo = (g_hi[q][:], g_lo[q][:]) if dest is None else dest
                nc.vector.tensor_tensor(lo, g[q][:], hi.bitcast(F32), ALU.subtract).then_inc(g_lo_done, 1)

            gated(1, 1, True)
            low(4, 0, PAIR_W)
            with dve.Fori(0, LOOP_ROUNDS) as i:
                for j in range(SLOTS):
                    p = SLOTS * i + (LOOP_FIRST + j)
                    gated(p, j % 2, True)
                    low(p + 3, (LOOP_FIRST + j + 3) % SLOTS, PAIR_W)
            for p in range(LOOP_END, PAIRS):
                gated(p, p % 2, True)
                if p + 3 < SAGE_L_SLAB:
                    low(p + 3, (p + 3) % SLOTS, slab_width(p + 3))
            dve.wait_ge(slab_used, SAGE_R_SLAB)
            for t in range(TILES):
                link(nc.vector.tensor_tensor(resid[:, t, :], resid[:, t, :], y[t][:], ALU.add))
                norm_stats(resid, t)
                if t == 1:
                    norm_apply(resid, 0, 3)
            norm_apply(resid, 1, 3)
            low_transposed(2)
            low(SAGE_L_SLAB, SAGE_L_SLAB % SLOTS, SLAB_W)
            for b in range(2):
                dve.wait_ge(zT_hi_done, 6 + b + 1)
                nc.vector.tensor_tensor(aggT_lo[:, 2 * b:2 * b + 2, :],
                                        gate_ps[b][:].rearrange("p (c n) -> p c n", c=2),
                                        aggT_hi[:, 2 * b:2 * b + 2, :].bitcast(F32), ALU.subtract).then_inc(zT_lo_done, 1)
            low(IN_SLAB, IN_SLAB % SLOTS, SLAB_W)
            dve.wait_ge(bias_added, 2 * TILES)
            for t, (ready, value) in enumerate(((sage_ready, 1), (slab_used, SAGE_R_SLAB + 1))):
                dve.wait_ge(ready, value)
                link(nc.vector.tensor_tensor(x[:, t, :], x[:, t, :], up_ps[t][:], ALU.add))

            dve.wait_ge(affine_in, 32)
            for t, (ready, value) in enumerate(((sage_ready, 2), (slab_used, SAGE_L_SLAB + 1))):
                dve.wait_ge(ready, value)
                link(nc.vector.scalar_tensor_tensor(resid[:, t, :], y[t][:], rdeg[:, t:t + 1], x[:, t, :],
                                                    ALU.mult, ALU.add))
                norm_stats(resid, t, 1.0 + LN_EPS, LN_EPS * LN_EPS)
                nc.vector.scalar_tensor_tensor(z[:, t, :], resid[:, t, :], mean_var[:, t, 0:1], ln_scale,
                                               ALU.subtract, ALU.mult).then_inc(scaled, 1)
                dve.wait_ge(rstd_ready, 3 * TILES + t + 1)
                dve.wait_ge(scaled, t + 1)
                nc.vector.scalar_tensor_tensor(z[:, t, :], z[:, t, :], rstd[:, t:t + 1], ln_bias,
                                               ALU.mult, ALU.add).then_inc(z_ready, 1)
            low_transposed(3)
            dve.wait_ge(logits_ready, 2)
            nc.vector.tensor_tensor(
                logits1[:], misc[1][:, 0:TILES * P].rearrange("p (t e) -> p t e", e=P)[:, :, EXPERTS:EXPERTS + GATES1],
                gate1_bias[:].unsqueeze(1).to_broadcast([P, TILES, GATES1]), ALU.add).then_inc(logits1_ready, 1)

            with dve.Fori(0, IN_SLABS // SLOTS) as i:
                for j in range(SLOTS):
                    for v in range(2):
                        unit = (2 * SLOTS) * i + (2 * j + v)
                        gated(PAIRS + unit, (PAIRS + v) % 2, False, source=pair_banks[(2 * j + v) % 4][1],
                              dest=(hid_hi[:, bass.ds(unit * TOKENS, TOKENS)], hid_lo[:, bass.ds(unit * TOKENS, TOKENS)]))
                    low(SLOTS * i + (IN_SLAB + SLOTS - 1 + j), (IN_SLAB - 1 + j) % SLOTS, SLAB_W)

            dve.wait_ge(logits1_ready, 1)
            nc.vector.tensor_tensor(group_on[:, :, 0], logits1[:, :, EXPERTS1], logits1[:, :, EXPERTS1 + 1],
                                    ALU.is_ge).then_inc(dve_chain, 1)
            chain[0] += 1
            link(nc.vector.tensor_tensor(group_on[:, :, 1], logits1[:, :, EXPERTS1 + 1], logits1[:, :, EXPERTS1],
                                         ALU.is_gt))
            link(nc.vector.tensor_scalar(group_pen[:], group_on[:], BIG, -BIG, ALU.mult, ALU.add))

            def spread_group(a, t):
                return a[:, t, :].unsqueeze(2).to_broadcast([P, GROUPS, EXPERTS1 // GROUPS])

            def by_group(a, t):
                return a[:, t, 0:EXPERTS1].rearrange("p (g e) -> p g e", g=GROUPS)

            for t in range(TILES):
                link(nc.vector.tensor_tensor(by_group(e1, t), by_group(logits1, t), spread_group(group_on, t), ALU.mult))
                link(nc.vector.tensor_tensor(by_group(e1, t), by_group(e1, t), spread_group(group_pen, t), ALU.add))
            link(nc.vector.tensor_reduce(neg_max[:], e1[:], axis=AX.X, op=ALU.max))
            nc.vector.tensor_tensor(e1[:], e1[:], neg_max[:].unsqueeze(2).to_broadcast([P, TILES, EXPERTS1]),
                                    ALU.subtract).then_inc(exp1_in, 1)
            dve.wait_ge(exp1_done, 1)
            link(nc.vector.tensor_reduce(exp_sum[:], p1[:], axis=AX.X, op=ALU.add))
            link(nc.vector.reciprocal(exp_rec[:], exp_sum[:]))
            link(nc.vector.tensor_tensor(p1[:], p1[:], exp_rec[:].unsqueeze(2).to_broadcast([P, TILES, EXPERTS1]), ALU.mult))
            link(nc.vector.tensor_scalar(group_pen[:], group_on[:], -1.0, None, ALU.add))
            for t in range(TILES):
                link(nc.vector.tensor_tensor(by_group(e1, t), by_group(p1, t), spread_group(group_pen, t), ALU.add))
                link(nc.vector.max(top[:, t, :], e1[:, t, :]))
                link(nc.vector.max_index(top_i[:, t, :], top[:, t, :], e1[:, t, :]))
            link(nc.vector.tensor_copy(top_f[:], top_i[:]))
            for t in range(TILES):
                link(nc.vector.tensor_tensor(hits1[:, t, :, :],
                                             iota_f[:, 0:EXPERTS1].unsqueeze(1).to_broadcast([P, 2, EXPERTS1]),
                                             top_f[:, t, 0:2].unsqueeze(2).to_broadcast([P, 2, EXPERTS1]), ALU.is_equal))
            dve.wait_ge(pool_const, 5)
            nc.vector.tensor_tensor(count1[:, :, 0:EXPERTS1], hits1[:, :, 0, :], hits1[:, :, 1, :],
                                    ALU.add).then_inc(count1_ready, 1)
            dve.wait_ge(count1_ready, 1)
            link(nc.vector.scalar_tensor_tensor(exp_sum[:], top[:, :, 0], 1e-8, top[:, :, 1], ALU.add, ALU.add))
            link(nc.vector.reciprocal(exp_rec[:], exp_sum[:]))
            link(nc.vector.tensor_tensor(comb1[:], p1[:], count1[:, :, 0:EXPERTS1], ALU.mult))
            link(nc.vector.tensor_tensor(comb1[:], comb1[:], exp_rec[:].unsqueeze(2).to_broadcast([P, TILES, EXPERTS1]),
                                         ALU.mult))

            for s in (OUT_SLAB + 3, OUT_SLAB + 4, OUT_SLAB + 5):
                low(s, s % SLOTS, SLAB_W)
            for t in range(TILES):
                dve.wait_ge(shared_ready, t + 1)
                nc.vector.tensor_tensor(resid[:, t, :], resid[:, t, :], pair_banks[0][t][:], ALU.add).then_inc(added, 1)

            def add_expert(e, q, signal):
                for t in range(TILES):
                    if t == 0:
                        dve.wait_ge(expert_ready, e + 1)
                    else:
                        dve.wait_ge(slab_used, 2 * e + used_value(OUT_SLAB + 3))
                    dve.wait_ge(added, TILES * e + (t + 1))
                    nc.vector.scalar_tensor_tensor(resid[:, t, :], pair_banks[1 - q][t][:],
                                                   comb1[:, t, bass.ds(e, 1)], resid[:, t, :],
                                                   ALU.mult, ALU.add).then_inc(signal, 1)

            with dve.Fori(0, 3) as i:
                for q in range(2):
                    for v in range(2):
                        n = 2 + 2 * q + v
                        low(SLOTS * i + (12 * SLOTS + n), n % SLOTS, SLAB_W)
                    add_expert(2 * i + q, q, added)
            add_expert(EXPERTS1 - 2, 0, added)
            add_expert(EXPERTS1 - 1, 1, result_ready)

        @block.tensor
        def _(pe):
            def product(dest, left, right, start, stop):
                (lh, ll), (rh, rl) = left, right
                nc.tensor.matmul(dest, lh, rh, start=start, stop=False)
                nc.tensor.matmul(dest, lh, rl, start=False, stop=False)
                return nc.tensor.matmul(dest, ll, rh, start=False, stop=stop)

            def parts(a, index):
                return a[0][index], a[1][index]

            def transpose_tokens(n):
                for t in range(TILES):
                    pe.wait_ge(z_ready, TILES * n + t + 1)
                    for c in range(CHUNKS):
                        last = nc.tensor.transpose(misc[t][:, c * P:(c + 1) * P], z[:, t, c * P:(c + 1) * P], ident[:])
                    last.then_inc(transposed, 1)

            activ, agg = (zT_hi, zT_lo), (aggT_hi, aggT_lo)

            def dense(dest, left, s, ready):
                slot = s % SLOTS
                pe.wait_ge(hi_done, s + 1)
                low_wait(pe, s)
                for t, signal in enumerate((ready, slab_used)):
                    dense_tile(dest[t], left, slot, t, signal)

            def dense_tile(dest, left, slot, t, signal):
                for c in range(CHUNKS):
                    last = product(dest[:], parts(left, (slice(None), c, slice(t * P, (t + 1) * P))),
                                   (w_hi[slot][:, c * FEATURES:(c + 1) * FEATURES],
                                    w_lo[slot][:, c * FEATURES:(c + 1) * FEATURES]), c == 0, c == CHUNKS - 1)
                last.then_inc(signal, 1)

            def gate_and_up(slot, offset, banks):
                for k, dest in enumerate(banks):
                    for c in range(CHUNKS):
                        at = offset + (k * CHUNKS + c) * P
                        last = product(dest[:, 0:TOKENS], (w_hi[slot][:, at:at + P], w_lo[slot][:, at:at + P]),
                                       parts(activ, (slice(None), c, slice(None))), c == 0, c == CHUNKS - 1)
                last.then_inc(up_ready, 1)
                return last

            def count_column(col, j, start, stop):
                pe.wait_ge(hot_ready, col + 1)
                for t in range(TILES):
                    last = nc.tensor.matmul(gate_ps[t][:, 0:TOKENS], hot_src[:, j, t * P:(t + 1) * P],
                                            hot_dst[:, j, :], start=start, stop=stop)
                last.then_inc(hot_used, 1)

            for j in range(BLOCK):
                count_column(j, j, j == 0, False)
            pe.wait_ge(pool_const, 2)
            transpose_tokens(0)
            with pe.Fori(0, BLOCKS - 2) as i:
                for j in range(BLOCK):
                    count_column(BLOCK * i + (BLOCK + j), j, False, False)
            for j in range(BLOCK):
                count_column(BLOCK * (BLOCKS - 1) + j, j, False, j == BLOCK - 1)
            for t in range(TILES):
                pe.wait_ge(count_copied, TILES)
                for s in range(TILES):
                    last = nc.tensor.transpose(up_ps[t][:, s * P:(s + 1) * P], count_t[:, s, t * P:(t + 1) * P], ident[:])
                last.then_inc(count_flipped, 1)
            pe.wait_ge(zT_hi_done, 2)
            pe.wait_ge(zT_lo_done, 2)
            dense(y, activ, GCN_SLAB, u_ps_ready)
            pe.wait_ge(deg_ready, TILES)
            pe.wait_ge(u_hi_done, TILES)
            pe.wait_ge(u_lo_done, TILES)
            for t in range(TILES):
                for s in range(TILES):
                    left = adj[:, s, t * P:(t + 1) * P]
                    nc.tensor.matmul(gate_ps[t][:], left, u_hi[:, s, :], start=s == 0, stop=False)
                    last = nc.tensor.matmul(gate_ps[t][:], left, u_lo[:, s, :], start=False, stop=s == TILES - 1)
                last.then_inc(gcn_ready, 1)
            transpose_tokens(1)
            pe.wait_ge(gates_hi_done, 1)
            pe.wait_ge(gates_lo_done, 1)

            def router(n):
                pe.wait_ge(zT_hi_done, TILES * n)
                pe.wait_ge(zT_lo_done, TILES * n)
                for c in range(CHUNKS):
                    last = product(misc[1][:, 0:TOKENS], parts((gates_hi, gates_lo), (slice(None), c, slice(None))),
                                   parts(activ, (slice(None), c, slice(None))), c == 0, c == CHUNKS - 1)
                last.then_inc(logitsT_ready, 1)

            def router_flip(n, dest):
                pe.wait_ge(logitsT_copied, n)
                for t in range(TILES):
                    last = nc.tensor.transpose(dest[:, t * P:(t + 1) * P], logitsT[:, t * P:(t + 1) * P], ident[:])
                last.then_inc(logits_ready, 1)

            router(2)
            def pair_in(p, slot, q, at=None):
                s = p + PAIR_SLAB
                pe.wait_ge(hi_done, s + 1)
                low_wait(pe, s, first=at)
                return gate_and_up(slot, 0, (gate_ps[q], up_ps[q]))

            def pair_spread(p, q):
                nc.tensor.matmul(misc[q][:, 0:TOKENS], pair_sel[:], comb_rows[:, bass.ds((p - 1) * TOKENS, TOKENS)],
                                 start=True, stop=True).then_inc(spread, 1)

            def pair_out(p, slot, q, start=False, stop=False):
                pe.wait_ge(g_lo_done, p + 1)
                for t in range(TILES):
                    last = product(y[t][:], (g_hi[q][:, t * P:(t + 1) * P], g_lo[q][:, t * P:(t + 1) * P]),
                                   (w_hi[slot][:, 2 * FEATURES:PAIR_W], w_lo[slot][:, 2 * FEATURES:PAIR_W]), start, stop)
                last.then_inc(slab_used, 1)
                return last

            router_flip(1, misc[0])
            pair_in(0, 1, 0)
            pair_in(1, 2, 1)
            pe.wait_ge(comb_hi_done, 1)
            pe.wait_ge(comb_lo_done, 1)
            for t in range(TILES):
                last = nc.tensor.transpose(misc[0][:, t * P:(t + 1) * P],
                                           comb_parts[:, t, :, :].rearrange("p a e -> p (a e)").bitcast(F32), ident[:])
            last.then_inc(combT_ps, 1)
            pair_out(0, 1, 0, start=True)
            pe.wait_ge(rows_in, 64)
            pe.wait_ge(pair_sel_done, 1)
            pair_spread(1, 1)
            pair_in(2, 3, 0)
            pair_spread(2, 0)
            pair_out(1, 2, 1)
            with pe.Fori(0, LOOP_ROUNDS) as i:
                for j in range(SLOTS):
                    p = SLOTS * i + (LOOP_FIRST + j)
                    slot = (LOOP_FIRST + j + PAIR_SLAB) % SLOTS
                    pair_in(p + 1, (slot + 1) % SLOTS, (j + 1) % 2, at=SLOTS)
                    pair_spread(p + 1, (j + 1) % 2)
                    pair_out(p, slot, j % 2)
            for p in range(LOOP_END, PAIRS):
                if p + 1 < PAIRS:
                    pair_in(p + 1, (p + 2) % SLOTS, (p + 1) % 2)
                    pair_spread(p + 1, (p + 1) % 2)
                pair_out(p, (p + 1) % SLOTS, p % 2, stop=p == PAIRS - 1)

            transpose_tokens(2)
            for b in range(2):
                for c in (2 * b, 2 * b + 1):
                    for s in range(TILES):
                        at = (c % 2) * TOKENS
                        last = nc.tensor.matmul(gate_ps[b][:, at:at + TOKENS], z[:, s, c * P:(c + 1) * P],
                                                count_t[:, s, :], start=s == 0, stop=s == TILES - 1)
                last.then_inc(agg_ready, 1)
            pe.wait_ge(zT_lo_done, 6)
            dense(up_ps, activ, SAGE_R_SLAB, sage_ready)
            pe.wait_ge(zT_lo_done, 8)
            dense(y, agg, SAGE_L_SLAB, sage_ready)

            transpose_tokens(3)
            router(5)
            router_flip(2, misc[1])

            with pe.Fori(0, IN_SLABS // SLOTS) as i:
                for j in range(SLOTS):
                    s = SLOTS * i + (IN_SLAB + j)
                    pe.wait_ge(hi_done, s + 1)
                    if j in (1, 2):
                        pe.wait_ge(pool_lo_done, SLOTS + j)
                    if j < SLOTS - 1:
                        pe.wait_ge(dve_lo_done, (j + 2) * i + (IN_SLAB - SLOTS + 1))
                    else:
                        pe.wait_ge(dve_lo_done, SLOTS * i + (IN_SLAB - SLOTS + 2))
                    for v in range(2):
                        k = (2 * SLOTS) * i + (PAIRS + 2 * j + v)
                        pe.wait_ge(g_lo_done, k - 3)
                        if (j, v) == (1, 1):
                            pe.wait_ge(logits1_ready, 1)
                        gate_and_up((IN_SLAB + j) % SLOTS, v * UNIT_W, pair_banks[(2 * j + v) % 4])

            def hidden(unit, t):
                at = unit * TOKENS + t * P
                return hid_hi[:, at:at + P], hid_lo[:, at:at + P]

            def out_half(first_unit, dest, s, slot, at, half, stop=True, ready=None):
                pe.wait_ge(hi_done, s + half + 1)
                low_wait(pe, s + half, first=at + half)
                for t in range(TILES):
                    for c in range(CHUNKS):
                        last = product(dest[t][:], hidden(first_unit + half * CHUNKS + c, t),
                                       (w_hi[slot + half][:, c * FEATURES:(c + 1) * FEATURES],
                                        w_lo[slot + half][:, c * FEATURES:(c + 1) * FEATURES]),
                                       half == 0 and c == 0, stop and half == 1 and c == CHUNKS - 1)
                    if t == 0 and ready is not None:
                        last.then_inc(ready, 1)
                last.then_inc(slab_used, 1)

            def expert_half(s, q, at, half):
                out_half(HIDDEN_CHUNKS, pair_banks[1 - q], s, at % SLOTS, at, half,
                         ready=expert_ready if half == 1 else None)

            def add_biases(dest):
                pe.wait_ge(count1_ready, 1)
                for n in range(TILES):
                    last = nc.tensor.transpose(misc[1][:, n * P:(n + 1) * P], count1[:, n, :], ident[:])
                last.then_inc(count1T_ps, 1)
                pe.wait_ge(count1T_ready, 1)
                for t in range(TILES):
                    nc.tensor.matmul(dest[t][:], count1T[:, t * P:(t + 1) * P], out_bias[:], start=False,
                                     stop=True).then_inc(shared_ready, 1)

            pe.wait_ge(g_lo_done, PAIRS + UNITS - 3)
            for half in range(2):
                out_half(0, pair_banks[0], OUT_SLAB, 0, OUT_SLAB, half, stop=False)
            pe.wait_ge(g_lo_done, PAIRS + UNITS)
            first = OUT_SLAB + 2
            expert_half(first, 0, first, 0)
            add_biases(pair_banks[0])
            expert_half(first, 0, first, 1)
            pe.wait_ge(added, TILES)
            for half in range(2):
                expert_half(first + 2, 1, first + 2, half)
            with pe.Fori(0, 3) as i:
                for q in range(2):
                    pe.wait_ge(added, 4 * i + (4 + 2 * q))
                    s = OUT_SLAB + 2 + 2 * (2 + q)
                    for half in range(2):
                        expert_half(SLOTS * i + s, q, s, half)


_OUT = ((TOKENS, FEATURES), "float32")


def _slabs(**a):
    import numpy as np

    def chunks(w):
        k, n = w.shape
        return w.reshape(k // P, P, n).transpose(1, 0, 2).reshape(P, -1)

    def pair_in(w):
        return w.reshape(PAIRS, 2, CHUNKS, P, 64).transpose(0, 3, 2, 1, 4).reshape(PAIRS, P, -1)

    def units(w):
        return w.reshape(2, HIDDEN_CHUNKS, P, CHUNKS, P).transpose(1, 4, 0, 3, 2).reshape(HIDDEN_CHUNKS, P, -1)

    def outs(w):
        e = w.shape[0]
        return w.transpose(0, 2, 1).reshape(e, 2, CHUNKS, P, FEATURES).transpose(0, 1, 3, 2, 4).reshape(2 * e, P, -1)

    u = np.concatenate([units(a["L1_ffn_shared_in_w"]), units(a["L1_ffn_expert_in_w"])])
    return {
        "x": a["x"], "src": a["src"], "dst": a["dst"],
        "gcn_w": chunks(a["L0_gnn_weight"]), "gcn_b": a["L0_gnn_bias"],
        "pairs": np.concatenate([pair_in(a["L0_ffn_w1"]), pair_in(a["L0_ffn_w3"]),
                                 a["L0_ffn_w2"].reshape(PAIRS, P, FEATURES)], axis=2),
        "gates": chunks(np.concatenate([a["L0_ffn_g_w"], a["L1_ffn_expert_gate_w"], a["L1_ffn_group_gate_w"]]).T)
        .reshape(P, CHUNKS, EXPERTS + GATES1),
        "gate_bias": a["L0_ffn_gate_bias"],
        "sage_r": chunks(a["L1_gnn_W_r"]), "sage_l": chunks(a["L1_gnn_W_l"]), "sage_b": a["L1_gnn_b"],
        "ln_scale": a["L1_ffn_ln_scale"], "ln_bias": a["L1_ffn_ln_bias"],
        "units": u.reshape(IN_SLABS, 2, P, UNIT_W).transpose(0, 2, 1, 3).reshape(IN_SLABS, P, SLAB_W),
        "outs": np.concatenate([outs(a["L1_ffn_shared_out_w"][None]), outs(a["L1_ffn_expert_out_weight"])]),
        "out_bias": np.concatenate([a["L1_ffn_expert_out_bias"], a["L1_ffn_shared_out_b"][None]]),
        "gate1_bias": np.concatenate([a["L1_ffn_expert_bias"], a["L1_ffn_group_bias"]]),
    }


def kernel(**inputs):
    import concourse.bacc as bacc
    import numpy as np
    from concourse.bass_utils import run_bass_kernel_spmd

    nc = bacc.Bacc("TRN2", target_bir_lowering=False, num_devices=1)
    arrays, args = {}, []
    for name, a in _slabs(**{k: np.asarray(v) for k, v in inputs.items()}).items():
        a = np.ascontiguousarray(a)
        arrays[f"in_{name}"] = a
        args.append(nc.dram_tensor(f"in_{name}", a.shape, mybir.dt.from_np(a.dtype), kind="ExternalInput").ap())
    args.append(nc.dram_tensor("out", _OUT[0], mybir.dt.from_np(np.dtype(_OUT[1])), kind="ExternalOutput").ap())
    build(nc, *args)
    return run_bass_kernel_spmd(nc, [arrays], core_ids=[0]).results[0]["out"]
```

```python
from contextlib import ExitStack

import concourse.bass as bass
from concourse import mybir

F32 = mybir.dt.float32
F32R = mybir.dt.float32r
BF16 = mybir.dt.bfloat16
I32 = mybir.dt.int32
U32 = mybir.dt.uint32
ALU = mybir.AluOpType
ACT = mybir.ActivationFunctionType
AX = mybir.AxisListType

P = 128
TOKENS, FEATURES, EDGES = 256, 512, 8192
TILES = TOKENS // P
CHUNKS = FEATURES // P
EDGE_COLS = EDGES // P
LN_EPS = 1e-5

EXPERTS, TOP_K, PAIRS, ROUTED_PAIRS = 64, 6, 33, 32
UNITS, HIDDEN_CHUNKS, EXPERTS1, GROUPS = 16, 8, 8, 2
GATES1 = EXPERTS1 + GROUPS

SLOTS = 4
SLAB_W = 2048
PAIR_W = 1536
UNIT_W = 1024
GCN_SLAB = 0
PAIR_SLAB = 1
SAGE_R_SLAB = PAIR_SLAB + PAIRS
SAGE_L_SLAB = SAGE_R_SLAB + 1
IN_SLAB = SAGE_L_SLAB + 1
IN_SLABS = UNITS // 2
OUT_SLAB = IN_SLAB + IN_SLABS
OUT_SLABS = 2 + 2 * EXPERTS1
SLABS = OUT_SLAB + OUT_SLABS

HOT_COLS, HOT_BUFS = 4, 4
HOT_GROUPS = EDGE_COLS // HOT_COLS
ACT_GROUPS = 2
DVE_GROUPS = HOT_GROUPS - ACT_GROUPS
LOOP_FIRST, LOOP_ROUNDS = 3, 6
LOOP_END = LOOP_FIRST + LOOP_ROUNDS * SLOTS

BIG = 1e30


def slab_width(s):
    return PAIR_W if PAIR_SLAB <= s < SAGE_R_SLAB else SLAB_W


def used_value(s):
    return s + 1 if s < IN_SLAB else s + 1 - IN_SLABS


def build(nc, x_in, src_in, dst_in, gcn_w_in, gcn_b_in, pairs_in, gates_in, gate_bias_in,
          sage_r_in, sage_l_in, sage_b_in, ln_scale_in, ln_bias_in, units_in, outs_in, out_bias_in,
          gate1_bias_in, out):
    with ExitStack() as ctx:
        def sb(name, shape, dt=F32):
            return ctx.enter_context(nc.sbuf_tensor(name, shape, dt))

        def sem(name):
            return ctx.enter_context(nc.semaphore(name))

        raw = [sb(f"raw{i}", [P, SLAB_W]) for i in range(SLOTS)]
        w_hi = [sb(f"w_hi{i}", [P, SLAB_W], F32R) for i in range(SLOTS)]
        w_lo = [sb(f"w_lo{i}", [P, SLAB_W], F32R) for i in range(SLOTS)]
        gates = sb("gates", [P, CHUNKS, P])
        gates_hi = sb("gates_hi", [P, CHUNKS, P], F32R)
        gates_lo = sb("gates_lo", [P, CHUNKS, P], F32R)
        gcn_b = sb("gcn_b", [P, FEATURES])
        sage_b = sb("sage_b", [P, FEATURES])
        gate_bias = sb("gate_bias", [P, EXPERTS])
        gate1_bias = sb("gate1_bias", [P, GATES1])
        out_bias = sb("out_bias", [EXPERTS1 + 1, FEATURES])
        ident = sb("ident", [P, P])
        diag = sb("diag", [P, TILES, TOKENS])
        iota_i = sb("iota_i", [P, TOKENS], I32)
        iota_b = sb("iota_b", [P, TOKENS, HOT_COLS], BF16)
        iota_f = sb("iota_f", [P, EXPERTS])
        table_load = sb("table_load", [P, TILES])
        minus_half = sb("minus_half", [P, TILES])
        pair_sel_f = sb("pair_sel_f", [4, P])
        pair_sel = sb("pair_sel", [4, P], F32R)
        ident_r = sb("ident_r", [P, P], F32R)
        edges_i = sb("edges_i", [P, 2, EDGE_COLS], I32)
        edges_b = sb("edges_b", [P, 2, EDGE_COLS], BF16)
        edges_f = sb("edges_f", [P, 2, ACT_GROUPS * HOT_COLS])
        hot_slots = range(2, SLOTS)
        hot = [raw[slot][:].bitcast(BF16).rearrange("p (b e n j) -> p b e n j", e=2, n=TOKENS, j=HOT_COLS)[:, b]
               for slot in hot_slots for b in range(HOT_BUFS // len(hot_slots))]
        count_t = sb("count_t", [P, TILES, TOKENS])
        both_ways = sb("both_ways", [P, TILES, TOKENS])
        ln_scale, ln_bias = (a[:].rearrange("p t n -> p (t n)") for a in (diag, both_ways))
        adj = sb("adj", [P, TILES, TOKENS], F32R)
        deg = sb("deg", [P, TILES])
        dinv = sb("dinv", [P, TILES])
        in_deg = sb("in_deg", [P, TILES])
        rdeg = sb("rdeg", [P, TILES])
        x = sb("x", [P, TILES, FEATURES])
        resid = sb("resid", [P, TILES, FEATURES])
        hot_act = [sb("hot_act", [P, 2, TOKENS, HOT_COLS], BF16),
                   resid[:].rearrange("p t f -> p (t f)").bitcast(BF16).rearrange("p (e n j) -> p e n j", e=2, j=HOT_COLS)]
        z = sb("z", [P, TILES, FEATURES])
        zT_hi = sb("zT_hi", [P, CHUNKS, TOKENS], F32R)
        zT_lo = sb("zT_lo", [P, CHUNKS, TOKENS], F32R)
        aggT_hi = sb("aggT_hi", [P, CHUNKS, TOKENS], F32R)
        aggT_lo = sb("aggT_lo", [P, CHUNKS, TOKENS], F32R)
        u_hi, u_lo = (a[:].rearrange("p c n -> p (c n)").rearrange("p (t f) -> p t f", t=TILES)
                      for a in (aggT_hi, aggT_lo))
        x1_hi, x1_lo = u_hi, u_lo
        logitsT = sb("logitsT", [P, TOKENS])
        stats = sb("stats", [P, TILES, 6])
        mean_var = sb("mean_var", [P, TILES, 2])
        var_eps = sb("var_eps", [P, TILES])
        rstd = sb("rstd", [P, TILES])
        top = sb("top", [P, TILES, 8])
        top_i = sb("top_i", [P, TILES, 8], U32)
        top_f = sb("top_f", [P, TILES, 8])
        neg_max = sb("neg_max", [P, TILES])
        exp_sum = sb("exp_sum", [P, TILES])
        exp_rec = sb("exp_rec", [P, TILES])
        probs = sb("probs", [P, TILES, EXPERTS])
        picked = sb("picked", [P, TILES, EXPERTS])
        replaced = sb("replaced", [P, TILES, EXPERTS])
        not_top = sb("not_top", [P, TILES, EXPERTS])
        comb = sb("comb", [P, TILES, EXPERTS])
        comb_parts = sb("comb_parts", [P, TILES, 2, 2, ROUTED_PAIRS], F32R)
        comb_by_place = comb[:].rearrange("p t (a k) -> p t k a", k=2)
        combT = sb("combT", [P, TOKENS], F32R)
        logits1 = sb("logits1", [P, TILES, GATES1])
        group_on = sb("group_on", [P, TILES, GROUPS])
        group_pen = sb("group_pen", [P, TILES, GROUPS])
        e1 = sb("e1", [P, TILES, EXPERTS1])
        p1 = sb("p1", [P, TILES, EXPERTS1])
        hits1 = sb("hits1", [P, TILES, 2, EXPERTS1])
        count1 = sb("count1", [P, TILES, P])
        count1T = sb("count1T", [EXPERTS1 + 1, TOKENS])
        comb1 = sb("comb1", [P, TILES, EXPERTS1])
        silu = [sb(f"silu{i}", [P, TOKENS]) for i in range(2)]
        glu = [sb(f"glu{i}", [P, TOKENS]) for i in range(2)]
        g = [sb(f"g{i}", [P, TOKENS]) for i in range(2)]
        g_hi = [sb(f"g_hi{i}", [P, TOKENS], F32R) for i in range(3)]
        g_lo = [sb(f"g_lo{i}", [P, TOKENS], F32R) for i in range(3)]
        hid = sb("hid", [P, 2 * UNITS * TOKENS], F32R)
        hid_hi, hid_lo = hid[:, 0:UNITS * TOKENS], hid[:, UNITS * TOKENS:]
        comb_rows = hid[0:4, 0:ROUTED_PAIRS * TOKENS]

        bank = [ctx.enter_context(nc.psum_tensor(f"bank{i}", [P, 512], F32)) for i in range(8)]
        y = bank[0:2]
        gate_ps = bank[2:4]
        up_ps = bank[4:6]
        misc = bank[6:8]
        pair_banks = [(gate_ps[0], up_ps[0]), (gate_ps[1], up_ps[1]), (y[0], y[1]), (misc[0], misc[1])]

        edges_in, x_in_s, consts_in = sem("edges_in"), sem("x_in"), sem("consts_in")
        raw_in = [sem(f"raw_in{i}") for i in range(SLOTS)]
        hi_done, gcn_lo_done, lo_done = sem("hi_done"), sem("gcn_lo_done"), sem("lo_done")
        slab_used = sem("slab_used")
        gates_hi_done, gates_lo_done = sem("gates_hi_done"), sem("gates_lo_done")
        pool_const, pool_chain, pad_done = sem("pool_const"), sem("pool_chain"), sem("pad_done")
        selectors_done = sem("selectors_done")
        x1_hi_done, x1_lo_done, x2_copied = sem("x1_hi_done"), sem("x1_lo_done"), sem("x2_copied")
        bias_added = sem("bias_added")
        var_ready, rstd_ready, z_ready = sem("var_ready"), sem("rstd_ready"), sem("z_ready")
        transposed, zT_hi_done, zT_lo_done = sem("transposed"), sem("zT_hi_done"), sem("zT_lo_done")
        affine_in, scaled = sem("affine_in"), sem("scaled")
        iota_b_done = sem("iota_b_done")
        hot_ready, hot_used = sem("hot_ready"), sem("hot_used")
        act_hot_used = sem("act_hot_used")
        edges_f_ready, distance_done, act_hot_ready = sem("edges_f_ready"), sem("distance_done"), sem("act_hot_ready")
        count_copied, count_flipped = sem("count_copied"), sem("count_flipped")
        deg_ready, dinv_ready = sem("deg_ready"), sem("dinv_ready")
        u_hi_done, u_lo_done = sem("u_hi_done"), sem("u_lo_done")
        u_ps_ready, gcn_ready = sem("u_ps_ready"), sem("gcn_ready")
        logitsT_ready, logitsT_copied = sem("logitsT_ready"), sem("logitsT_copied")
        logits_ready, max_ready, exp_ready = sem("logits_ready"), sem("max_ready"), sem("exp_ready")
        comb_ready, comb_hi_done, comb_lo_done = sem("comb_ready"), sem("comb_hi_done"), sem("comb_lo_done")
        combT_ps, combT_ready, rows_in = sem("combT_ps"), sem("combT_ready"), sem("rows_in")
        up_ready, silu_done, glu_done = sem("up_ready"), sem("silu_done"), sem("glu_done")
        spread, g_done, g_hi_done, g_lo_done = sem("spread"), sem("g_done"), sem("g_hi_done"), sem("g_lo_done")
        agg_ready = sem("agg_ready")
        sage_ready = sem("sage_ready")
        logits1_ready = sem("logits1_ready")
        exp1_in, exp1_done = sem("exp1_in"), sem("exp1_done")
        count1_ready, count1T_ps, count1T_ready = sem("count1_ready"), sem("count1T_ps"), sem("count1T_ready")
        shared_ready, expert_ready, added = sem("shared_ready"), sem("expert_ready"), sem("added")
        dve_chain = sem("dve_chain")
        result_ready, stored = sem("result_ready"), sem("stored")

        block = ctx.enter_context(nc.Block())

        def g_parts(p):
            return 2 if p == PAIRS - 1 else p % 2

        def tile_of(a, t):
            return a[:, :, t * P:(t + 1) * P]

        def low_wait(eng, s):
            eng.wait_ge(lo_done, s)

        @block.sync
        def _(sp):
            def load(slot, source, width):
                sp.dma_start(raw[slot][:, 0:width], source).then_inc(raw_in[slot], 16)

            sp.dma_start(edges_i[:, 0, :], src_in.rearrange("(p j) -> p j", p=P)).then_inc(edges_in, 16)
            sp.dma_start(x[:], x_in.rearrange("(t p) f -> p t f", p=P)).then_inc(x_in_s, 16)
            load(0, gcn_w_in, SLAB_W)
            for s in range(PAIR_SLAB, 2 * SLOTS):
                if s == hot_slots[0]:
                    sp.wait_ge(hot_used, DVE_GROUPS)
                elif s == SLOTS:
                    sp.wait_ge(gcn_lo_done, 1)
                elif s > SLOTS:
                    low_wait(sp, s - SLOTS)
                load(s % SLOTS, pairs_in[s - PAIR_SLAB], PAIR_W)
            with sp.Fori(0, 6) as i:
                for j in range(SLOTS):
                    s = 2 * SLOTS + SLOTS * i + j
                    low_wait(sp, s - SLOTS)
                    load(j, pairs_in[bass.ds(s - PAIR_SLAB, 1), :, :].rearrange("a p w -> p (a w)"), PAIR_W)
            sp.wait_ge(deg_ready, TILES)
            sp.dma_start(ln_scale, ln_scale_in.partition_broadcast(P)).then_inc(affine_in, 16)
            sp.dma_start(ln_bias, ln_bias_in.partition_broadcast(P)).then_inc(affine_in, 16)
            for s in range(8 * SLOTS, 12 * SLOTS):
                low_wait(sp, s - SLOTS)
                if s < SAGE_R_SLAB:
                    load(s % SLOTS, pairs_in[s - PAIR_SLAB], PAIR_W)
                elif s == SAGE_R_SLAB:
                    load(s % SLOTS, sage_r_in, SLAB_W)
                elif s == SAGE_L_SLAB:
                    load(s % SLOTS, sage_l_in, SLAB_W)
                elif s < OUT_SLAB:
                    load(s % SLOTS, units_in[s - IN_SLAB], SLAB_W)
                else:
                    load(s % SLOTS, outs_in[s - OUT_SLAB], SLAB_W)
            with sp.Fori(0, 3) as i:
                for j in range(SLOTS):
                    s = 12 * SLOTS + SLOTS * i + j
                    low_wait(sp, s - SLOTS)
                    load(j, outs_in[bass.ds(s - OUT_SLAB, 1), :, :].rearrange("a p w -> p (a w)"), SLAB_W)
            for s in range(15 * SLOTS, SLABS):
                low_wait(sp, s - SLOTS)
                load(s % SLOTS, outs_in[s - OUT_SLAB], SLAB_W)
            for t in range(TILES):
                sp.wait_ge(result_ready, t + 1)
                sp.dma_start(out[t * P:(t + 1) * P, :], resid[:, t, :]).then_inc(stored, 16)
            sp.wait_ge(stored, 16 * TILES)

        @block.gpsimd
        def _(pool):
            chain = [0]

            def link(ins):
                chain[0] += 1
                ins.then_inc(pool_chain, 1)
                pool.wait_ge(pool_chain, chain[0])

            nc.gpsimd.iota(iota_i[:], [[1, TOKENS]], base=0, channel_multiplier=0).then_inc(pool_const, 1)
            link(nc.gpsimd.memset(ident[:], 0.0))
            nc.gpsimd.affine_select(out=ident[:], in_=ident[:], compare_op=ALU.not_equal, fill=1.0, base=0,
                                    pattern=[[-1, P]], channel_multiplier=1).then_inc(pool_const, 1)
            link(nc.gpsimd.memset(minus_half[:], -0.5))
            nc.gpsimd.memset(gates[:], 0.0).then_inc(pad_done, 1)

            def inverse_roots(n):
                for t in range(TILES):
                    pool.wait_ge(var_ready, TILES * (n - 1) + t + 1)
                    nc.gpsimd.tensor_tensor(rstd[:, t:t + 1], var_eps[:, t:t + 1], minus_half[:, t:t + 1],
                                            ALU.pow).then_inc(rstd_ready, 1)

            inverse_roots(1)
            pool.wait_ge(hi_done, GCN_SLAB + 1)
            nc.gpsimd.tensor_tensor(w_lo[0][:], raw[0][:], w_hi[0][:].bitcast(F32), ALU.subtract).then_inc(gcn_lo_done, 1)
            nc.gpsimd.tensor_copy(iota_f[:], iota_i[:, 0:EXPERTS]).then_inc(pool_const, 1)
            link(nc.gpsimd.memset(diag[:], 0.0))
            nc.gpsimd.affine_select(out=diag[:], in_=diag[:], compare_op=ALU.not_equal, fill=1.0, base=0,
                                    pattern=[[P, TILES], [-1, TOKENS]], channel_multiplier=1).then_inc(pool_const, 1)
            link(nc.gpsimd.memset(pair_sel_f[:], 1.0))
            link(nc.gpsimd.affine_select(out=pair_sel_f[:, 0:64], in_=pair_sel_f[:, 0:64], compare_op=ALU.is_ge,
                                         fill=0.0, base=1, pattern=[[0, 64]], channel_multiplier=-1))
            link(nc.gpsimd.affine_select(out=pair_sel_f[:, 64:P], in_=pair_sel_f[:, 64:P], compare_op=ALU.is_ge,
                                         fill=0.0, base=-2, pattern=[[0, 64]], channel_multiplier=1))
            nc.gpsimd.tensor_copy(pair_sel[:], pair_sel_f[:]).then_inc(selectors_done, 1)
            nc.gpsimd.tensor_copy(ident_r[:], ident[:]).then_inc(selectors_done, 1)
            nc.gpsimd.memset(count1[:], 1.0).then_inc(pool_const, 1)

            pool.wait_ge(gates_hi_done, 1)
            nc.gpsimd.tensor_tensor(gates_lo[:], gates[:], gates_hi[:].bitcast(F32), ALU.subtract).then_inc(gates_lo_done, 1)
            pool.wait_ge(x_in_s, 16)
            pool.wait_ge(consts_in, 16 * 6)
            pool.wait_ge(act_hot_used, ACT_GROUPS)
            for t in range(TILES):
                nc.gpsimd.tensor_tensor(resid[:, t, :], x[:, t, :], gcn_b[:], ALU.add).then_inc(bias_added, 1)
            pool.wait_ge(deg_ready, TILES)
            nc.gpsimd.tensor_tensor(dinv[:], deg[:], minus_half[:], ALU.pow).then_inc(dinv_ready, 1)

            inverse_roots(2)
            inverse_roots(3)
            for t in range(TILES):
                pool.wait_ge(x2_copied, t + 1)
                nc.gpsimd.tensor_tensor(x[:, t, :], resid[:, t, :], sage_b[:], ALU.add).then_inc(bias_added, 1)
            inverse_roots(4)

        @block.scalar
        def _(act):
            act.dma_start(edges_i[:, 1, :], dst_in.rearrange("(p j) -> p j", p=P)).then_inc(edges_in, 16)
            act.dma_start(gcn_b[:], gcn_b_in.partition_broadcast(P)).then_inc(consts_in, 16)
            act.wait_ge(pad_done, 1)
            act.dma_start(gates[:, :, 0:EXPERTS + GATES1], gates_in).then_inc(consts_in, 16)
            nc.scalar.activation(table_load[:], minus_half[:], ACT.Copy)
            act.dma_start(gate_bias[:], gate_bias_in.partition_broadcast(P)).then_inc(consts_in, 16)
            act.dma_start(sage_b[:], sage_b_in.partition_broadcast(P)).then_inc(consts_in, 16)
            act.dma_start(gate1_bias[:], gate1_bias_in.partition_broadcast(P)).then_inc(consts_in, 16)
            act.dma_start(out_bias[:], out_bias_in).then_inc(consts_in, 16)

            def high(s, slot, width, used=None):
                act.wait_ge(raw_in[slot], (s - slot) * (16 // SLOTS) + 16)
                if used is not None:
                    act.wait_ge(slab_used, used)
                nc.scalar.activation(w_hi[slot][:, 0:width], raw[slot][:, 0:width], ACT.Copy).then_inc(hi_done, 1)

            def split_tile(n, t):
                act.wait_ge(transposed, TILES * n + t + 1)
                nc.scalar.activation(tile_of(zT_hi, t), misc[t][:].rearrange("p (c n) -> p c n", c=CHUNKS),
                                     ACT.Copy).then_inc(zT_hi_done, 1)

            def split_transposed(n):
                for t in range(TILES):
                    split_tile(n, t)

            def copy_logits(n):
                act.wait_ge(logitsT_ready, n)
                nc.scalar.activation(logitsT[:], misc[0][:, 0:TOKENS], ACT.Copy).then_inc(logitsT_copied, 1)

            def distances(n):
                for e in range(2):
                    for j in range(HOT_COLS):
                        col = n * HOT_COLS + j
                        last = nc.scalar.activation(hot_act[n][:, e, :, j], iota_b[:, :, 0], ACT.Abs,
                                                    bias=edges_f[:, e, col:col + 1], scale=-1.0)
                last.then_inc(distance_done, 1)

            def act_hot_group(n):
                act.wait_ge(distance_done, n + 1)
                nc.scalar.activation(hot_act[n][:], hot_act[n][:], ACT.Relu, bias=1.0, scale=-1.0).then_inc(act_hot_ready, 1)

            act.wait_ge(iota_b_done, 1)
            act.wait_ge(edges_f_ready, 1)
            distances(0)
            high(0, 0, SLAB_W)
            split_transposed(0)
            act_hot_group(0)
            act.wait_ge(consts_in, 16 * 6)
            nc.scalar.activation(gates_hi[:], gates[:], ACT.Copy).then_inc(gates_hi_done, 1)
            distances(1)
            act_hot_group(1)
            high(PAIR_SLAB, PAIR_SLAB, PAIR_W)
            for t in range(TILES):
                act.wait_ge(hot_used, DVE_GROUPS)
                act.wait_ge(act_hot_used, ACT_GROUPS)
                nc.scalar.activation(count_t[:, t, :], gate_ps[t][:, 0:TOKENS], ACT.Copy).then_inc(count_copied, 1)
            for t, ready in enumerate((u_ps_ready, slab_used)):
                act.wait_ge(ready, 1)
                act.wait_ge(dinv_ready, 1)
                nc.scalar.activation(u_hi[:, t, :], y[t][:], ACT.Copy, scale=dinv[:, t:t + 1]).then_inc(u_hi_done, 1)
            for s in range(PAIR_SLAB + 1, SLOTS):
                high(s, s, PAIR_W)
            split_transposed(1)
            copy_logits(1)

            def act_silu(k, q, source=None):
                act.wait_ge(up_ready, k + 1)
                nc.scalar.activation(silu[q][:], (source or gate_ps[q])[:, 0:TOKENS], ACT.Silu).then_inc(silu_done, 1)

            def act_g_high(k, q, dest=None):
                act.wait_ge(g_done, k + 1)
                nc.scalar.activation(g_hi[q][:] if dest is None else dest, g[q][:], ACT.Copy).then_inc(g_hi_done, 1)

            for t in range(TILES):
                act.wait_ge(max_ready, 1)
                nc.scalar.activation(probs[:, t, :], misc[1][:, t * P:t * P + EXPERTS], ACT.Exp,
                                     bias=neg_max[:, t:t + 1], accum_out=exp_sum[:, t:t + 1]).then_inc(exp_ready, 1)
            act_silu(0, 0)
            act.wait_ge(comb_ready, TILES)
            nc.scalar.activation(comb_parts[:, :, :, 0, :], comb_by_place, ACT.Copy).then_inc(comb_hi_done, 1)
            act_g_high(0, 0)
            act.wait_ge(combT_ps, 1)
            nc.scalar.activation(combT[:], misc[0][:, 0:TOKENS], ACT.Copy).then_inc(combT_ready, 1)
            act.wait_ge(combT_ready, 1)
            act.dma_start(comb_rows.bitcast(F32).rearrange("r (a n) -> r a n", n=TOKENS),
                          combT[:].bitcast(F32)).then_inc(rows_in, 16)
            act_silu(1, 1)
            high(4, 0, PAIR_W, used=1)
            act_g_high(1, 1)
            high(5, 1, PAIR_W, used=2)
            act_silu(2, 0)
            act_g_high(2, 0)
            high(6, 2, PAIR_W, used=3)
            with act.Fori(0, LOOP_ROUNDS) as i:
                for j in range(SLOTS):
                    p = SLOTS * i + (LOOP_FIRST + j)
                    act_silu(p, (LOOP_FIRST + j) % 2)
                    act_g_high(p, (LOOP_FIRST + j) % 2)
                    high(p + 4, (LOOP_FIRST + j) % SLOTS, PAIR_W, used=p + 1)
            for p in range(LOOP_END, PAIRS):
                act_silu(p, p % 2)
                act_g_high(p, p % 2, g_hi[g_parts(p)][:])
                if p < PAIRS - 2:
                    high(p + 4, (p + 4) % SLOTS, slab_width(p + 4), used=p + 1)
                if p < LOOP_END + TILES:
                    t = p - LOOP_END
                    nc.scalar.activation(x1_hi[:, t, :], resid[:, t, :], ACT.Copy).then_inc(x1_hi_done, 1)
            for s in (SAGE_L_SLAB, IN_SLAB):
                high(s, s % SLOTS, SLAB_W, used=used_value(s - SLOTS))
            for t in range(TILES):
                act.wait_ge(z_ready, 2 * TILES + t + 1)
                nc.scalar.activation(resid[:, t, :], y[t][:], ACT.Copy).then_inc(x2_copied, 1)
                split_tile(2, t)
            for b in range(2):
                act.wait_ge(agg_ready, b + 1)
                nc.scalar.activation(aggT_hi[:, 2 * b:2 * b + 2, :],
                                     gate_ps[b][:].rearrange("p (c n) -> p c n", c=2), ACT.Copy).then_inc(zT_hi_done, 1)
            high(IN_SLAB + 1, (IN_SLAB + 1) % SLOTS, SLAB_W, used=used_value(IN_SLAB - 3))
            for t, s in enumerate((IN_SLAB + 2, IN_SLAB + 3)):
                split_tile(3, t)
                high(s, s % SLOTS, SLAB_W, used=used_value(s - SLOTS))
            copy_logits(2)
            with act.Fori(0, IN_SLABS // SLOTS) as i:
                for j in range(SLOTS):
                    for v in range(2):
                        unit = (2 * SLOTS) * i + (2 * j + v)
                        act_silu(PAIRS + unit, (PAIRS + v) % 2, pair_banks[(2 * j + v) % 4][0])
                        act_g_high(PAIRS + unit, (PAIRS + v) % 2, hid_hi[:, bass.ds(unit * TOKENS, TOKENS)])
                    high(SLOTS * i + (IN_SLAB + SLOTS + j), (IN_SLAB + j) % SLOTS, SLAB_W)
            act.wait_ge(exp1_in, 1)
            nc.scalar.activation(p1[:], e1[:], ACT.Exp).then_inc(exp1_done, 1)
            high(12 * SLOTS, 0, SLAB_W, used=used_value(11 * SLOTS))
            act.wait_ge(count1T_ps, 1)
            nc.scalar.activation(count1T[:], misc[1][0:EXPERTS1 + 1, 0:TOKENS], ACT.Copy).then_inc(count1T_ready, 1)
            with act.Fori(0, 3) as i:
                for j in range(1, SLOTS + 1):
                    high(SLOTS * i + (12 * SLOTS + j), j % SLOTS, SLAB_W, used=SLOTS * i + used_value(11 * SLOTS + j))
            for s in range(15 * SLOTS + 1, SLABS):
                high(s, s % SLOTS, SLAB_W, used=used_value(s - SLOTS))

        @block.vector
        def _(dve):
            chain = [0]

            def link(ins):
                chain[0] += 1
                ins.then_inc(dve_chain, 1)
                dve.wait_ge(dve_chain, chain[0])

            def count(ins):
                chain[0] += 1
                ins.then_inc(dve_chain, 1)
                return chain[0]

            def done(value):
                dve.wait_ge(dve_chain, value)

            def norm_stats(source, t, factor=1.0, eps=LN_EPS):
                link(nc.vector.bn_stats(stats[:, t, :], source))
                link(nc.vector.bn_aggr(mean_var[:, t, :], stats[:, t, :]))
                nc.vector.tensor_scalar(var_eps[:, t:t + 1], mean_var[:, t, 1:2], factor, eps, ALU.mult,
                                        ALU.add).then_inc(var_ready, 1)

            def norm_apply(source, t, n):
                dve.wait_ge(rstd_ready, TILES * (n - 1) + t + 1)
                nc.vector.tensor_scalar(z[:, t, :], source, mean_var[:, t, 0:1], rstd[:, t:t + 1],
                                        ALU.subtract, ALU.mult).then_inc(z_ready, 1)

            def low(s, slot, width):
                dve.wait_ge(hi_done, s + 1)
                nc.vector.tensor_tensor(w_lo[slot][:, 0:width], raw[slot][:, 0:width],
                                        w_hi[slot][:, 0:width].bitcast(F32), ALU.subtract).then_inc(lo_done, 1)

            def low_transposed(n, tiles=range(TILES)):
                for t in tiles:
                    dve.wait_ge(zT_hi_done, TILES * (n if n < 3 else n + 1) + t + 1)
                    nc.vector.tensor_tensor(tile_of(zT_lo, t), misc[t][:].rearrange("p (c n) -> p c n", c=CHUNKS),
                                            tile_of(zT_hi, t).bitcast(F32), ALU.subtract).then_inc(zT_lo_done, 1)

            dve.wait_ge(pool_const, 1)
            nc.vector.tensor_copy(iota_b[:], iota_i[:].unsqueeze(2).to_broadcast([P, TOKENS, HOT_COLS])).then_inc(iota_b_done, 1)
            dve.wait_ge(edges_in, 32)
            link(nc.vector.tensor_copy(edges_b[:], edges_i[:]))

            def hot_group(group, b):
                nc.vector.tensor_tensor(
                    hot[b],
                    edges_b[:, :, group * HOT_COLS:(group + 1) * HOT_COLS].unsqueeze(2).to_broadcast([P, 2, TOKENS, HOT_COLS]),
                    iota_b[:].unsqueeze(1).to_broadcast([P, 2, TOKENS, HOT_COLS]), ALU.is_equal).then_inc(hot_ready, 1)

            dve.wait_ge(iota_b_done, 1)
            for b in range(HOT_BUFS):
                hot_group(b, b)
                if b == 0:
                    nc.vector.tensor_copy(edges_f[:], edges_i[:, :, DVE_GROUPS * HOT_COLS:]).then_inc(edges_f_ready, 1)
                if b == 1:
                    dve.wait_ge(x_in_s, 16)
                    for t in range(TILES):
                        norm_stats(x[:, t, :], t)
                elif b == 2:
                    for t in range(TILES):
                        norm_apply(x[:, t, :], t, 1)
            for group in range(HOT_BUFS, DVE_GROUPS):
                dve.wait_ge(hot_used, group - HOT_BUFS + 1)
                hot_group(group, group % HOT_BUFS)
                if group == HOT_BUFS + 1:
                    low_transposed(0)
            dve.wait_ge(pool_const, 4)
            for t in range(TILES):
                dve.wait_ge(count_copied, t + 1)
                dve.wait_ge(count_flipped, t + 1)
                link(nc.vector.tensor_tensor(both_ways[:, t, :], up_ps[t][:, 0:TOKENS], count_t[:, t, :], ALU.add))
                nc.vector.scalar_tensor_tensor(adj[:, t, :], both_ways[:, t, :], 1.0, diag[:, t, :], ALU.min, ALU.add,
                                               accum_out=deg[:, t:t + 1]).then_inc(deg_ready, 1)
            for t in range(TILES):
                link(nc.vector.tensor_reduce(in_deg[:, t:t + 1], up_ps[t][:, 0:TOKENS], axis=AX.X, op=ALU.add))
            link(nc.vector.tensor_scalar(in_deg[:], in_deg[:], 1.0, None, ALU.max))
            link(nc.vector.reciprocal(rdeg[:], in_deg[:]))
            dve.wait_ge(dinv_ready, 1)
            for t in range(TILES):
                dve.wait_ge(u_hi_done, t + 1)
                nc.vector.scalar_tensor_tensor(u_lo[:, t, :], y[t][:], dinv[:, t:t + 1], u_hi[:, t, :].bitcast(F32),
                                               ALU.mult, ALU.subtract).then_inc(u_lo_done, 1)
            low(PAIR_SLAB, PAIR_SLAB, PAIR_W)
            dve.wait_ge(bias_added, TILES)

            def add_gcn(t):
                dve.wait_ge(gcn_ready, t + 1)
                return nc.vector.scalar_tensor_tensor(resid[:, t, :], gate_ps[t][:], dinv[:, t:t + 1], resid[:, t, :],
                                                      ALU.mult, ALU.add)

            link(add_gcn(0))
            norm_stats(resid[:, 0, :], 0)
            tile_1 = count(add_gcn(1))
            norm_apply(resid[:, 0, :], 0, 2)
            done(tile_1)
            norm_stats(resid[:, 1, :], 1)
            norm_apply(resid[:, 1, :], 1, 2)
            low_transposed(1)
            low(PAIR_SLAB + 1, PAIR_SLAB + 1, PAIR_W)

            dve.wait_ge(logits_ready, 1)
            scores = misc[1][:, 0:TILES * P].rearrange("p (t e) -> p t e", e=P)[:, :, 0:EXPERTS]
            link(nc.vector.tensor_reduce(neg_max[:], scores, axis=AX.X, op=ALU.max))
            nc.vector.tensor_scalar(neg_max[:], neg_max[:], -1.0, None, ALU.mult).then_inc(max_ready, 1)
            dve.wait_ge(exp_ready, TILES)
            link(nc.vector.reciprocal(exp_rec[:], exp_sum[:]))
            step = [count(nc.vector.scalar_tensor_tensor(picked[:, t, :], probs[:, t, :], exp_rec[:, t:t + 1],
                                                         gate_bias[:], ALU.mult, ALU.add)) for t in range(TILES)]
            after = []
            for t in range(TILES):
                done(step[t])
                after.append(count(nc.vector.max(top[:, t, :], picked[:, t, :])))
            step = after
            after = []
            for t in range(TILES):
                done(step[t])
                after.append(count(nc.vector.max_index(top_i[:, t, :], top[:, t, :], picked[:, t, :])))
            replaced_at = [count(nc.vector.match_replace(replaced[:, t, :], top[:, t, :], picked[:, t, :], -BIG))
                           for t in range(TILES)]
            done(after[1])
            cast = count(nc.vector.tensor_copy(top_f[:], top_i[:]))
            after = []
            for t in range(TILES):
                done(replaced_at[t])
                after.append(count(nc.vector.tensor_tensor(replaced[:, t, :], replaced[:, t, :], picked[:, t, :],
                                                           ALU.not_equal)))
            step = after
            done(cast)
            after = []
            for t in range(TILES):
                done(step[t])
                after.append(count(nc.vector.scalar_tensor_tensor(
                    not_top[:, t, :], iota_f[:], top_f[:, t, TOP_K:TOP_K + 1], replaced[:, t, :],
                    ALU.is_equal, ALU.subtract)))
            step = after
            after = []
            for t in range(TILES):
                done(step[t])
                after.append(count(nc.vector.scalar_tensor_tensor(
                    replaced[:, t, :], iota_f[:], top_f[:, t, TOP_K + 1:TOP_K + 2], not_top[:, t, :],
                    ALU.is_equal, ALU.add)))
            step = after
            link(nc.vector.tensor_scalar(exp_rec[:], exp_rec[:], -1.0, None, ALU.mult))
            for t in range(TILES):
                done(step[t])
                nc.vector.scalar_tensor_tensor(comb[:, t, :], probs[:, t, :], exp_rec[:, t:t + 1], replaced[:, t, :],
                                               ALU.mult, ALU.mult).then_inc(comb_ready, 1)
            dve.wait_ge(silu_done, 1)
            nc.vector.tensor_tensor(g[0][:], silu[0][:], up_ps[0][:, 0:TOKENS], ALU.mult).then_inc(g_done, 1)
            dve.wait_ge(comb_hi_done, 1)
            nc.vector.tensor_tensor(comb_parts[:, :, :, 1, :], comb_by_place, comb_parts[:, :, :, 0, :].bitcast(F32),
                                    ALU.subtract).then_inc(comb_lo_done, 1)
            dve.wait_ge(g_hi_done, 1)
            nc.vector.tensor_tensor(g_lo[0][:], g[0][:], g_hi[0][:].bitcast(F32), ALU.subtract).then_inc(g_lo_done, 1)

            def multiply(p, q):
                dve.wait_ge(silu_done, p + 1)
                nc.vector.tensor_tensor(glu[q][:], silu[q][:], up_ps[q][:, 0:TOKENS], ALU.mult).then_inc(glu_done, 1)

            def split_g(k, hi, lo, q):
                dve.wait_ge(g_hi_done, k + 1)
                nc.vector.tensor_tensor(lo, g[q][:], hi.bitcast(F32), ALU.subtract).then_inc(g_lo_done, 1)

            def weigh(p, q, parts=None):
                dve.wait_ge(spread, p)
                dve.wait_ge(glu_done, p)
                nc.vector.tensor_tensor(g[q][:], glu[q][:], misc[q][:, 0:TOKENS], ALU.mult).then_inc(g_done, 1)
                parts = q if parts is None else parts
                split_g(p, g_hi[parts][:], g_lo[parts][:], q)

            low(PAIR_SLAB + 2, PAIR_SLAB + 2, PAIR_W)
            multiply(1, 1)
            low(4, 0, PAIR_W)
            weigh(1, 1)
            multiply(2, 0)
            weigh(2, 0)
            low(5, 1, PAIR_W)
            with dve.Fori(0, LOOP_ROUNDS) as i:
                for j in range(SLOTS):
                    p = SLOTS * i + (LOOP_FIRST + j)
                    multiply(p, (LOOP_FIRST + j) % 2)
                    weigh(p, (LOOP_FIRST + j) % 2)
                    low(p + 3, (LOOP_FIRST + j + 3) % SLOTS, PAIR_W)
            for p in range(LOOP_END, PAIRS):
                multiply(p, p % 2)
                weigh(p, p % 2, g_parts(p))
                if p + 3 < SAGE_L_SLAB:
                    low(p + 3, (p + 3) % SLOTS, slab_width(p + 3))
                if LOOP_END < p <= LOOP_END + TILES:
                    t = p - LOOP_END - 1
                    dve.wait_ge(x1_hi_done, t + 1)
                    nc.vector.tensor_tensor(x1_lo[:, t, :], resid[:, t, :], x1_hi[:, t, :].bitcast(F32),
                                            ALU.subtract).then_inc(x1_lo_done, 1)
            dve.wait_ge(slab_used, SAGE_R_SLAB)
            for t in range(TILES):
                norm_stats(y[t][:], t)
            for t in range(TILES):
                norm_apply(y[t][:], t, 3)
            low_transposed(2)
            low(SAGE_L_SLAB, SAGE_L_SLAB % SLOTS, SLAB_W)
            for b in range(2):
                dve.wait_ge(zT_hi_done, 6 + b + 1)
                nc.vector.tensor_tensor(aggT_lo[:, 2 * b:2 * b + 2, :],
                                        gate_ps[b][:].rearrange("p (c n) -> p c n", c=2),
                                        aggT_hi[:, 2 * b:2 * b + 2, :].bitcast(F32), ALU.subtract).then_inc(zT_lo_done, 1)
            low(IN_SLAB, IN_SLAB % SLOTS, SLAB_W)
            dve.wait_ge(bias_added, 2 * TILES)
            dve.wait_ge(affine_in, 32)
            for t in range(TILES):
                dve.wait_ge(*((sage_ready, 1), (slab_used, SAGE_R_SLAB + 1))[t])
                link(nc.vector.tensor_tensor(x[:, t, :], x[:, t, :], up_ps[t][:], ALU.add))
                if t == 1:
                    low_transposed(3, (0,))
                dve.wait_ge(*((sage_ready, 2), (slab_used, SAGE_L_SLAB + 1))[t])
                link(nc.vector.scalar_tensor_tensor(resid[:, t, :], y[t][:], rdeg[:, t:t + 1], x[:, t, :],
                                                    ALU.mult, ALU.add))
                norm_stats(resid[:, t, :], t, 1.0 + LN_EPS, LN_EPS * LN_EPS)
                nc.vector.scalar_tensor_tensor(z[:, t, :], resid[:, t, :], mean_var[:, t, 0:1], ln_scale,
                                               ALU.subtract, ALU.mult).then_inc(scaled, 1)
                dve.wait_ge(rstd_ready, 3 * TILES + t + 1)
                dve.wait_ge(scaled, t + 1)
                nc.vector.scalar_tensor_tensor(z[:, t, :], z[:, t, :], rstd[:, t:t + 1], ln_bias,
                                               ALU.mult, ALU.add).then_inc(z_ready, 1)
            low_transposed(3, (1,))
            for s in (IN_SLAB + 1, IN_SLAB + 2):
                low(s, s % SLOTS, SLAB_W)
            dve.wait_ge(logits_ready, 2)
            nc.vector.tensor_tensor(
                logits1[:], misc[1][:, 0:TILES * P].rearrange("p (t e) -> p t e", e=P)[:, :, EXPERTS:EXPERTS + GATES1],
                gate1_bias[:].unsqueeze(1).to_broadcast([P, TILES, GATES1]), ALU.add).then_inc(logits1_ready, 1)

            with dve.Fori(0, IN_SLABS // SLOTS) as i:
                for j in range(SLOTS):
                    for v in range(2):
                        unit = (2 * SLOTS) * i + (2 * j + v)
                        q = (PAIRS + v) % 2
                        dve.wait_ge(silu_done, unit + (PAIRS + 1))
                        nc.vector.tensor_tensor(g[q][:], silu[q][:], pair_banks[(2 * j + v) % 4][1][:, 0:TOKENS],
                                                ALU.mult).then_inc(g_done, 1)
                        split_g(PAIRS + unit, hid_hi[:, bass.ds(unit * TOKENS, TOKENS)],
                                hid_lo[:, bass.ds(unit * TOKENS, TOKENS)], q)
                    low(SLOTS * i + (IN_SLAB + SLOTS - 1 + j), (IN_SLAB - 1 + j) % SLOTS, SLAB_W)

            dve.wait_ge(logits1_ready, 1)
            nc.vector.tensor_tensor(group_on[:, :, 0], logits1[:, :, EXPERTS1], logits1[:, :, EXPERTS1 + 1],
                                    ALU.is_ge).then_inc(dve_chain, 1)
            chain[0] += 1
            link(nc.vector.tensor_tensor(group_on[:, :, 1], logits1[:, :, EXPERTS1 + 1], logits1[:, :, EXPERTS1],
                                         ALU.is_gt))
            link(nc.vector.tensor_scalar(group_pen[:], group_on[:], BIG, -BIG, ALU.mult, ALU.add))

            def spread_group(a, t):
                return a[:, t, :].unsqueeze(2).to_broadcast([P, GROUPS, EXPERTS1 // GROUPS])

            def by_group(a, t):
                return a[:, t, 0:EXPERTS1].rearrange("p (g e) -> p g e", g=GROUPS)

            for t in range(TILES):
                link(nc.vector.tensor_tensor(by_group(e1, t), by_group(logits1, t), spread_group(group_on, t), ALU.mult))
                link(nc.vector.tensor_tensor(by_group(e1, t), by_group(e1, t), spread_group(group_pen, t), ALU.add))
            link(nc.vector.tensor_reduce(neg_max[:], e1[:], axis=AX.X, op=ALU.max))
            nc.vector.tensor_tensor(e1[:], e1[:], neg_max[:].unsqueeze(2).to_broadcast([P, TILES, EXPERTS1]),
                                    ALU.subtract).then_inc(exp1_in, 1)
            dve.wait_ge(exp1_done, 1)
            link(nc.vector.tensor_reduce(exp_sum[:], p1[:], axis=AX.X, op=ALU.add))
            link(nc.vector.reciprocal(exp_rec[:], exp_sum[:]))
            link(nc.vector.tensor_tensor(p1[:], p1[:], exp_rec[:].unsqueeze(2).to_broadcast([P, TILES, EXPERTS1]), ALU.mult))
            link(nc.vector.tensor_scalar(group_pen[:], group_on[:], -1.0, None, ALU.add))
            for t in range(TILES):
                link(nc.vector.tensor_tensor(by_group(e1, t), by_group(p1, t), spread_group(group_pen, t), ALU.add))
                link(nc.vector.max(top[:, t, :], e1[:, t, :]))
                link(nc.vector.max_index(top_i[:, t, :], top[:, t, :], e1[:, t, :]))
            link(nc.vector.tensor_copy(top_f[:], top_i[:]))
            for t in range(TILES):
                link(nc.vector.tensor_tensor(hits1[:, t, :, :],
                                             iota_f[:, 0:EXPERTS1].unsqueeze(1).to_broadcast([P, 2, EXPERTS1]),
                                             top_f[:, t, 0:2].unsqueeze(2).to_broadcast([P, 2, EXPERTS1]), ALU.is_equal))
            dve.wait_ge(pool_const, 5)
            nc.vector.tensor_tensor(count1[:, :, 0:EXPERTS1], hits1[:, :, 0, :], hits1[:, :, 1, :],
                                    ALU.add).then_inc(count1_ready, 1)
            dve.wait_ge(count1_ready, 1)
            link(nc.vector.scalar_tensor_tensor(exp_sum[:], top[:, :, 0], 1e-8, top[:, :, 1], ALU.add, ALU.add))
            link(nc.vector.reciprocal(exp_rec[:], exp_sum[:]))
            link(nc.vector.tensor_tensor(comb1[:], p1[:], count1[:, :, 0:EXPERTS1], ALU.mult))
            link(nc.vector.tensor_tensor(comb1[:], comb1[:], exp_rec[:].unsqueeze(2).to_broadcast([P, TILES, EXPERTS1]),
                                         ALU.mult))

            for s in (OUT_SLAB + 3, OUT_SLAB + 4, OUT_SLAB + 5):
                low(s, s % SLOTS, SLAB_W)
            for t in range(TILES):
                dve.wait_ge(shared_ready, t + 1)
                nc.vector.tensor_tensor(resid[:, t, :], resid[:, t, :], pair_banks[0][t][:], ALU.add).then_inc(added, 1)

            def add_expert(e, q, signal):
                for t in range(TILES):
                    if t == 0:
                        dve.wait_ge(expert_ready, e + 1)
                    else:
                        dve.wait_ge(slab_used, 2 * e + used_value(OUT_SLAB + 3))
                    dve.wait_ge(added, TILES * e + (t + 1))
                    nc.vector.scalar_tensor_tensor(resid[:, t, :], pair_banks[1 - q][t][:],
                                                   comb1[:, t, bass.ds(e, 1)], resid[:, t, :],
                                                   ALU.mult, ALU.add).then_inc(signal, 1)

            with dve.Fori(0, 3) as i:
                for q in range(2):
                    for v in range(2):
                        n = 2 + 2 * q + v
                        low(SLOTS * i + (12 * SLOTS + n), n % SLOTS, SLAB_W)
                    add_expert(2 * i + q, q, added)
            add_expert(EXPERTS1 - 2, 0, added)
            add_expert(EXPERTS1 - 1, 1, result_ready)

        @block.tensor
        def _(pe):
            def product(dest, left, right, start, stop):
                (lh, ll), (rh, rl) = left, right
                nc.tensor.matmul(dest, lh, rh, start=start, stop=False)
                nc.tensor.matmul(dest, lh, rl, start=False, stop=False)
                return nc.tensor.matmul(dest, ll, rh, start=False, stop=stop)

            def parts(a, index):
                return a[0][index], a[1][index]

            def keep_clock(dest, n):
                for _ in range(n):
                    nc.tensor.matmul(dest[:], gates_hi[:, 0, :], gates_hi[:].rearrange("p c n -> p (c n)"),
                                     start=True, stop=True)

            def transpose_tile(n, t):
                pe.wait_ge(z_ready, TILES * n + t + 1)
                for c in range(CHUNKS):
                    last = nc.tensor.transpose(misc[t][:, c * P:(c + 1) * P], z[:, t, c * P:(c + 1) * P], ident[:])
                last.then_inc(transposed, 1)

            def transpose_tokens(n):
                for t in range(TILES):
                    transpose_tile(n, t)

            activ, agg = (zT_hi, zT_lo), (aggT_hi, aggT_lo)

            def slab_wait(s):
                pe.wait_ge(hi_done, s + 1)
                low_wait(pe, s)

            def dense_tile(dest, left, slot, t, signal, chunks=range(CHUNKS)):
                for c in chunks:
                    last = product(dest[:], parts(left, (slice(None), c, slice(t * P, (t + 1) * P))),
                                   (w_hi[slot][:, c * FEATURES:(c + 1) * FEATURES],
                                    w_lo[slot][:, c * FEATURES:(c + 1) * FEATURES]), c == 0, c == CHUNKS - 1)
                if signal is not None:
                    last.then_inc(signal, 1)

            def gate_and_up(slot, offset, banks):
                for k, dest in enumerate(banks):
                    for c in range(CHUNKS):
                        at = offset + (k * CHUNKS + c) * P
                        last = product(dest[:, 0:TOKENS], (w_hi[slot][:, at:at + P], w_lo[slot][:, at:at + P]),
                                       parts(activ, (slice(None), c, slice(None))), c == 0, c == CHUNKS - 1)
                last.then_inc(up_ready, 1)

            def count_group(columns, used, start=False, stop=False):
                for j in range(HOT_COLS):
                    for t in range(TILES):
                        last = nc.tensor.matmul(gate_ps[t][:, 0:TOKENS], columns[:, 0, t * P:(t + 1) * P, j],
                                                columns[:, 1, :, j], start=start and j == 0,
                                                stop=stop and j == HOT_COLS - 1)
                last.then_inc(used, 1)

            def count_act_group(n):
                pe.wait_ge(act_hot_ready, n + 1)
                count_group(hot_act[n], act_hot_used, stop=n == ACT_GROUPS - 1)

            for group in range(DVE_GROUPS):
                if group == HOT_BUFS - 1:
                    pe.wait_ge(pool_const, 2)
                    transpose_tokens(0)
                elif group == HOT_BUFS + 2:
                    pe.wait_ge(zT_hi_done, 2)
                    pe.wait_ge(zT_lo_done, 2)
                    pe.wait_ge(hi_done, GCN_SLAB + 1)
                    pe.wait_ge(gcn_lo_done, 1)
                    dense_tile(y[0], activ, 0, 0, None, chunks=range(2))
                elif group == DVE_GROUPS - 5:
                    count_act_group(0)
                pe.wait_ge(hot_ready, group + 1)
                count_group(hot[group % HOT_BUFS], hot_used, start=group == 0)
            count_act_group(1)
            dense_tile(y[0], activ, 0, 0, None, chunks=range(2, 3))
            for t in range(TILES):
                pe.wait_ge(count_copied, TILES)
                for s in range(TILES):
                    last = nc.tensor.transpose(up_ps[t][:, s * P:(s + 1) * P], count_t[:, s, t * P:(t + 1) * P], ident[:])
                last.then_inc(count_flipped, 1)
            dense_tile(y[0], activ, 0, 0, u_ps_ready, chunks=range(3, CHUNKS))
            dense_tile(y[1], activ, 0, 1, slab_used)
            pe.wait_ge(deg_ready, TILES)
            for s in range(TILES):
                for part, ready in ((u_hi, u_hi_done), (u_lo, u_lo_done)):
                    pe.wait_ge(ready, s + 1)
                    for t in range(TILES):
                        last_part = s == TILES - 1 and part is u_lo
                        done = nc.tensor.matmul(gate_ps[t][:], adj[:, s, t * P:(t + 1) * P], part[:, s, :],
                                                start=s == 0 and part is u_hi, stop=last_part)
                        if last_part:
                            done.then_inc(gcn_ready, 1)
            pe.wait_ge(gates_hi_done, 1)
            keep_clock(y[0], 16)
            transpose_tile(1, 0)
            keep_clock(y[0], 6)
            transpose_tile(1, 1)
            keep_clock(y[0], 6)
            pe.wait_ge(gates_lo_done, 1)

            def router(parts_made):
                pe.wait_ge(zT_hi_done, parts_made)
                pe.wait_ge(zT_lo_done, parts_made)
                for c in range(CHUNKS):
                    last = product(misc[0][:, 0:TOKENS], parts((gates_hi, gates_lo), (slice(None), c, slice(None))),
                                   parts(activ, (slice(None), c, slice(None))), c == 0, c == CHUNKS - 1)
                last.then_inc(logitsT_ready, 1)

            def router_flip(n):
                pe.wait_ge(logitsT_copied, n)
                for t in range(TILES):
                    last = nc.tensor.transpose(misc[1][:, t * P:(t + 1) * P], logitsT[:, t * P:(t + 1) * P], ident[:])
                last.then_inc(logits_ready, 1)

            router(4)
            def pair_in(p, slot, q):
                slab_wait(p + PAIR_SLAB)
                gate_and_up(slot, 0, (gate_ps[q], up_ps[q]))

            def pair_spread(p, q):
                nc.tensor.matmul(misc[q][:, 0:TOKENS], pair_sel[:], comb_rows[:, bass.ds((p - 1) * TOKENS, TOKENS)],
                                 start=True, stop=True).then_inc(spread, 1)

            def pair_out(p, slot, q, start=False, stop=False):
                pe.wait_ge(g_lo_done, p + 1)
                for t in range(TILES):
                    last = product(y[t][:], (g_hi[q][:, t * P:(t + 1) * P], g_lo[q][:, t * P:(t + 1) * P]),
                                   (w_hi[slot][:, 2 * FEATURES:PAIR_W], w_lo[slot][:, 2 * FEATURES:PAIR_W]), start, stop)
                last.then_inc(slab_used, 1)
                return last

            router_flip(1)
            pair_in(0, PAIR_SLAB, 0)
            pair_in(1, 2, 1)
            pe.wait_ge(comb_hi_done, 1)
            pe.wait_ge(comb_lo_done, 1)
            for t in range(TILES):
                last = nc.tensor.transpose(misc[0][:, t * P:(t + 1) * P],
                                           comb_parts[:, t].rearrange("p k part a -> p (k part a)").bitcast(F32), ident[:])
            last.then_inc(combT_ps, 1)
            pair_out(0, 1, 0, start=True)
            pair_in(2, 3, 0)
            pe.wait_ge(rows_in, 16)
            pe.wait_ge(selectors_done, 2)
            pair_spread(1, 1)
            pair_spread(2, 0)
            pe.wait_ge(glu_done, 1)
            pair_in(3, 0, 1)
            pair_out(1, 2, 1)
            pair_spread(3, 1)
            pair_out(2, 3, 0)
            with pe.Fori(0, LOOP_ROUNDS) as i:
                for j in range(SLOTS):
                    p = SLOTS * i + (LOOP_FIRST + j)
                    slot = (LOOP_FIRST + j + PAIR_SLAB) % SLOTS
                    q = (LOOP_FIRST + j) % 2
                    pair_in(p + 1, (slot + 1) % SLOTS, 1 - q)
                    pair_spread(p + 1, 1 - q)
                    pair_out(p, slot, q)
            for p in range(LOOP_END, PAIRS - 3):
                pair_in(p + 1, (p + 2) % SLOTS, (p + 1) % 2)
                pair_spread(p + 1, (p + 1) % 2)
                pair_out(p, (p + 1) % SLOTS, p % 2)
            pair_in(PAIRS - 2, (PAIRS - 1) % SLOTS, (PAIRS - 2) % 2)
            pair_spread(PAIRS - 2, (PAIRS - 2) % 2)
            pe.wait_ge(glu_done, PAIRS - 3)
            pair_in(PAIRS - 1, PAIRS % SLOTS, (PAIRS - 1) % 2)
            pair_out(PAIRS - 3, (PAIRS - 2) % SLOTS, (PAIRS - 3) % 2)
            pair_spread(PAIRS - 1, (PAIRS - 1) % 2)
            pair_out(PAIRS - 2, (PAIRS - 1) % SLOTS, g_parts(PAIRS - 2))
            pe.wait_ge(x1_hi_done, TILES)
            pe.wait_ge(x1_lo_done, TILES)
            for t in range(TILES):
                for part in (x1_hi, x1_lo):
                    nc.tensor.matmul(y[t][:], ident_r[:], part[:, t, :], start=False, stop=False)
            pair_out(PAIRS - 1, PAIRS % SLOTS, g_parts(PAIRS - 1), stop=True)

            keep_clock(up_ps[1], 13)
            transpose_tile(2, 0)
            keep_clock(up_ps[1], 1)
            transpose_tile(2, 1)
            for b in range(2):
                for c in (2 * b, 2 * b + 1):
                    for s in range(TILES):
                        at = (c % 2) * TOKENS
                        last = nc.tensor.matmul(gate_ps[b][:, at:at + TOKENS], z[:, s, c * P:(c + 1) * P],
                                                count_t[:, s, :], start=s == 0, stop=s == TILES - 1)
                last.then_inc(agg_ready, 1)
            pe.wait_ge(zT_lo_done, 6)
            r_slot, l_slot = SAGE_R_SLAB % SLOTS, SAGE_L_SLAB % SLOTS
            slab_wait(SAGE_R_SLAB)
            dense_tile(up_ps[0], activ, r_slot, 0, sage_ready)
            pe.wait_ge(zT_lo_done, 8)
            slab_wait(SAGE_L_SLAB)
            dense_tile(y[0], agg, l_slot, 0, sage_ready)
            dense_tile(up_ps[1], activ, r_slot, 1, slab_used)
            dense_tile(y[1], agg, l_slot, 1, None, chunks=range(CHUNKS // 2))
            transpose_tile(3, 0)
            dense_tile(y[1], agg, l_slot, 1, slab_used, chunks=range(CHUNKS // 2, CHUNKS))

            keep_clock(gate_ps[0], 16)
            transpose_tile(3, 1)
            keep_clock(gate_ps[0], 6)
            router(10)
            keep_clock(gate_ps[0], 3)
            router_flip(2)
            with pe.Fori(0, IN_SLABS // SLOTS) as i:
                for j in range(SLOTS):
                    slab_wait(SLOTS * i + (IN_SLAB + j))
                    for v in range(2):
                        k = (2 * SLOTS) * i + (PAIRS + 2 * j + v)
                        pe.wait_ge(g_lo_done, k - 3)
                        if (j, v) == (1, 1):
                            pe.wait_ge(logits1_ready, 1)
                        gate_and_up((IN_SLAB + j) % SLOTS, v * UNIT_W, pair_banks[(2 * j + v) % 4])

            def hidden(unit, t):
                at = unit * TOKENS + t * P
                return hid_hi[:, at:at + P], hid_lo[:, at:at + P]

            def out_half(first_unit, dest, s, slot, half, stop=True, ready=None, between=None):
                slab_wait(s + half)
                for t in range(TILES):
                    for c in range(CHUNKS):
                        last = product(dest[t][:], hidden(first_unit + half * CHUNKS + c, t),
                                       (w_hi[slot + half][:, c * FEATURES:(c + 1) * FEATURES],
                                        w_lo[slot + half][:, c * FEATURES:(c + 1) * FEATURES]),
                                       half == 0 and c == 0, stop and half == 1 and c == CHUNKS - 1)
                    if t == 0 and ready is not None:
                        last.then_inc(ready, 1)
                    if t == 0 and between is not None:
                        between()
                last.then_inc(slab_used, 1)

            def expert_half(s, slot, q, half, between=None):
                out_half(HIDDEN_CHUNKS, pair_banks[1 - q], s, slot, half, ready=expert_ready if half == 1 else None,
                         between=between)

            def flip_counts():
                pe.wait_ge(count1_ready, 1)
                for n in range(TILES):
                    last = nc.tensor.transpose(misc[1][:, n * P:(n + 1) * P], count1[:, n, :], ident[:])
                last.then_inc(count1T_ps, 1)

            def add_biases(dest):
                pe.wait_ge(count1T_ready, 1)
                for t in range(TILES):
                    nc.tensor.matmul(dest[t][:], count1T[:, t * P:(t + 1) * P], out_bias[:], start=False,
                                     stop=True).then_inc(shared_ready, 1)

            pe.wait_ge(g_lo_done, PAIRS + UNITS - 3)
            for half in range(2):
                out_half(0, pair_banks[0], OUT_SLAB, 0, half, stop=False)
            pe.wait_ge(g_lo_done, PAIRS + UNITS)
            first = OUT_SLAB + 2
            expert_half(first, first % SLOTS, 0, 0, between=flip_counts)
            add_biases(pair_banks[0])
            expert_half(first, first % SLOTS, 0, 1)
            pe.wait_ge(added, TILES)
            for half in range(2):
                expert_half(first + 2, (first + 2) % SLOTS, 1, half)
            with pe.Fori(0, 3) as i:
                for q in range(2):
                    pe.wait_ge(added, 4 * i + (4 + 2 * q))
                    s = OUT_SLAB + 2 + 2 * (2 + q)
                    for half in range(2):
                        expert_half(SLOTS * i + s, s % SLOTS, q, half)


_OUT = ((TOKENS, FEATURES), "float32")


def _slabs(**a):
    import numpy as np

    def chunks(w):
        k, n = w.shape
        return w.reshape(k // P, P, n).transpose(1, 0, 2).reshape(P, -1)

    def pair_in(w):
        return w.reshape(PAIRS, 2, CHUNKS, P, 64).transpose(0, 3, 2, 1, 4).reshape(PAIRS, P, -1)

    def units(w):
        return w.reshape(2, HIDDEN_CHUNKS, P, CHUNKS, P).transpose(1, 4, 0, 3, 2).reshape(HIDDEN_CHUNKS, P, -1)

    def outs(w):
        e = w.shape[0]
        return w.transpose(0, 2, 1).reshape(e, 2, CHUNKS, P, FEATURES).transpose(0, 1, 3, 2, 4).reshape(2 * e, P, -1)

    u = np.concatenate([units(a["L1_ffn_shared_in_w"]), units(a["L1_ffn_expert_in_w"])])
    return {
        "x": a["x"], "src": a["src"], "dst": a["dst"],
        "gcn_w": chunks(a["L0_gnn_weight"]), "gcn_b": a["L0_gnn_bias"],
        "pairs": np.concatenate([pair_in(a["L0_ffn_w1"]), pair_in(a["L0_ffn_w3"]),
                                 a["L0_ffn_w2"].reshape(PAIRS, P, FEATURES)], axis=2),
        "gates": chunks(np.concatenate([a["L0_ffn_g_w"], a["L1_ffn_expert_gate_w"], a["L1_ffn_group_gate_w"]]).T)
        .reshape(P, CHUNKS, EXPERTS + GATES1),
        "gate_bias": a["L0_ffn_gate_bias"],
        "sage_r": chunks(a["L1_gnn_W_r"]), "sage_l": chunks(a["L1_gnn_W_l"]), "sage_b": a["L1_gnn_b"],
        "ln_scale": a["L1_ffn_ln_scale"], "ln_bias": a["L1_ffn_ln_bias"],
        "units": u.reshape(IN_SLABS, 2, P, UNIT_W).transpose(0, 2, 1, 3).reshape(IN_SLABS, P, SLAB_W),
        "outs": np.concatenate([outs(a["L1_ffn_shared_out_w"][None]), outs(a["L1_ffn_expert_out_weight"])]),
        "out_bias": np.concatenate([a["L1_ffn_expert_out_bias"], a["L1_ffn_shared_out_b"][None]]),
        "gate1_bias": np.concatenate([a["L1_ffn_expert_bias"], a["L1_ffn_group_bias"]]),
    }


def kernel(**inputs):
    import concourse.bacc as bacc
    import numpy as np
    from concourse.bass_utils import run_bass_kernel_spmd

    nc = bacc.Bacc("TRN2", target_bir_lowering=False, num_devices=1)
    arrays, args = {}, []
    for name, a in _slabs(**{k: np.asarray(v) for k, v in inputs.items()}).items():
        a = np.ascontiguousarray(a)
        arrays[f"in_{name}"] = a
        args.append(nc.dram_tensor(f"in_{name}", a.shape, mybir.dt.from_np(a.dtype), kind="ExternalInput").ap())
    args.append(nc.dram_tensor("out", _OUT[0], mybir.dt.from_np(np.dtype(_OUT[1])), kind="ExternalOutput").ap())
    build(nc, *args)
    return run_bass_kernel_spmd(nc, [arrays], core_ids=[0]).results[0]["out"]
```
